# Optimizing a Trainium2 kernel written in Bass

```python
import numpy as np
import jax
import jax.numpy as jnp

def _softmax(x, axis=-1):
    return jax.nn.softmax(x, axis=axis)

def _gelu(x):
    return jax.nn.gelu(x, approximate=True)

def _silu(x):
    return jax.nn.silu(x)

def _sigmoid(x):
    return jax.nn.sigmoid(x)

def _layernorm(x, axis=-1, eps=1e-05):
    m = jnp.mean(x, axis=axis, keepdims=True)
    v = jnp.var(x, axis=axis, keepdims=True)
    return (x - m) / jnp.sqrt(v + eps)

def _scatter_add(tgt, idx, src, axis=0):
    return tgt.at[idx].add(src)

def _segment_sum(src, seg, n):
    return jax.ops.segment_sum(src, seg, n)
kernel_name = 'mk_seq_postln_d2_jaxref_r8_20d063'

def setup_inputs(seed: int=0):
    np.random.seed(seed)
    _w = jnp.asarray

    def _L0_attn_setup():
        import jax, jax.numpy as jnp
        import numpy as np
        NUM_HEADS = 16
        NUM_KV_HEADS = 4
        ROPE_BASE = 10000.0

        def _rotate_half(x):
            x1 = x[..., ::2]
            x2 = x[..., 1::2]
            return jnp.stack((-x2, x1), axis=-1).reshape(x.shape)

        def apply_rope(x, positions, base):
            head_dim = x.shape[-1]
            inv_freq = 1.0 / base ** (jnp.arange(0, head_dim, 2, dtype=jnp.float32) / head_dim)
            freqs = positions.astype(jnp.float32)[:, None] * inv_freq[None, :]
            cos = jnp.repeat(jnp.cos(freqs), 2, axis=-1)[None, :, None, :]
            sin = jnp.repeat(jnp.sin(freqs), 2, axis=-1)[None, :, None, :]
            return x * cos + _rotate_half(x) * sin
        key = jax.random.key(seed)
        ks = jax.random.split(key, 9)
        B, S, H = (2, 256, 256)
        kvdim = NUM_KV_HEADS * (H // NUM_HEADS)
        s = 0.02
        return {'x': jax.random.normal(ks[0], (B, S, H), jnp.float32), 'Wq': jax.random.normal(ks[1], (H, H), jnp.float32) * s, 'bq': jnp.zeros((H,), jnp.float32), 'Wk': jax.random.normal(ks[2], (kvdim, H), jnp.float32) * s, 'bk': jnp.zeros((kvdim,), jnp.float32), 'Wv': jax.random.normal(ks[3], (kvdim, H), jnp.float32) * s, 'bv': jnp.zeros((kvdim,), jnp.float32), 'Wo': jax.random.normal(ks[4], (H, H), jnp.float32) * s, 'bo': jnp.zeros((H,), jnp.float32)}
    _L0_attn_in = _L0_attn_setup()

    def _L0_ffn_setup():
        import jax, jax.numpy as jnp
        import numpy as np
        B, S, H, I = (1, 64, 256, 768)

        def _quantized_matmul(x, w, scale):
            wq = w.astype(jnp.float8_e4m3fn).astype(x.dtype)
            y = jnp.einsum('bsi,io->bso', x, wq)
            return y * scale
        key = jax.random.key(seed)
        ks = jax.random.split(key, 7)
        return {'x': jax.random.normal(ks[0], (B, S, H), dtype=jnp.float32), 'gate_w': jax.random.normal(ks[1], (H, I), dtype=jnp.float32) * 0.02, 'up_w': jax.random.normal(ks[2], (H, I), dtype=jnp.float32) * 0.02, 'down_w': jax.random.normal(ks[3], (I, H), dtype=jnp.float32) * 0.02, 'gate_scale': jax.random.uniform(ks[4], (I,), dtype=jnp.float32, minval=0.5, maxval=1.5), 'up_scale': jax.random.uniform(ks[5], (I,), dtype=jnp.float32, minval=0.5, maxval=1.5), 'down_scale': jax.random.uniform(ks[6], (H,), dtype=jnp.float32, minval=0.5, maxval=1.5)}
    _L0_ffn_in = _L0_ffn_setup()

    def _L1_attn_setup():
        import jax, jax.numpy as jnp
        import numpy as np
        D_MODEL = 256
        N_HEADS = 16
        HEAD_DIM = D_MODEL // N_HEADS
        BATCH = 2
        SEQ = 256
        key = jax.random.key(seed)
        kx, kq, kk, kv, ko = jax.random.split(key, 5)
        s = 1.0 / np.sqrt(D_MODEL)
        return {'x': jax.random.normal(kx, (BATCH, SEQ, D_MODEL), dtype=jnp.float32), 'wq': jax.random.normal(kq, (D_MODEL, D_MODEL), dtype=jnp.float32) * s, 'wk': jax.random.normal(kk, (D_MODEL, D_MODEL), dtype=jnp.float32) * s, 'wv': jax.random.normal(kv, (D_MODEL, D_MODEL), dtype=jnp.float32) * s, 'wo': jax.random.normal(ko, (D_MODEL, D_MODEL), dtype=jnp.float32) * s}
    _L1_attn_in = _L1_attn_setup()

    def _L1_ffn_setup():
        import jax, jax.numpy as jnp
        import numpy as np
        DIM_IN = 256
        DIM_HIDDEN = 1024
        key = jax.random.key(seed)
        k_x, k_g, k_u, k_d = jax.random.split(key, 4)
        s_in = 1.0 / np.sqrt(DIM_IN)
        s_hid = 1.0 / np.sqrt(DIM_HIDDEN)
        x = jax.random.normal(k_x, (4, 256, DIM_IN), dtype=jnp.float32)
        w_gate = jax.random.uniform(k_g, (DIM_HIDDEN, DIM_IN), jnp.float32, -s_in, s_in)
        w_up = jax.random.uniform(k_u, (DIM_HIDDEN, DIM_IN), jnp.float32, -s_in, s_in)
        w_down = jax.random.uniform(k_d, (DIM_IN, DIM_HIDDEN), jnp.float32, -s_hid, s_hid)
        return {'x': x, 'w_gate': w_gate, 'w_up': w_up, 'w_down': w_down}
    _L1_ffn_in = _L1_ffn_setup()
    _d = {'L0_attn_x': _L0_attn_in['x'], 'L0_attn_Wq': _L0_attn_in['Wq'], 'L0_attn_bq': _L0_attn_in['bq'], 'L0_attn_Wk': _L0_attn_in['Wk'], 'L0_attn_bk': _L0_attn_in['bk'], 'L0_attn_Wv': _L0_attn_in['Wv'], 'L0_attn_bv': _L0_attn_in['bv'], 'L0_attn_Wo': _L0_attn_in['Wo'], 'L0_attn_bo': _L0_attn_in['bo'], 'L0_ffn_gate_w': _L0_ffn_in['gate_w'], 'L0_ffn_up_w': _L0_ffn_in['up_w'], 'L0_ffn_down_w': _L0_ffn_in['down_w'], 'L0_ffn_gate_scale': _L0_ffn_in['gate_scale'], 'L0_ffn_up_scale': _L0_ffn_in['up_scale'], 'L0_ffn_down_scale': _L0_ffn_in['down_scale'], 'L1_attn_wq': _L1_attn_in['wq'], 'L1_attn_wk': _L1_attn_in['wk'], 'L1_attn_wv': _L1_attn_in['wv'], 'L1_attn_wo': _L1_attn_in['wo'], 'L1_ffn_w_gate': _L1_ffn_in['w_gate'], 'L1_ffn_w_up': _L1_ffn_in['w_up'], 'L1_ffn_w_down': _L1_ffn_in['w_down']}
    _x0 = _d['L0_attn_x']
    _d['L0_attn_x'] = jax.random.normal(jax.random.fold_in(jax.random.key(seed), 1), (1, 2048, 256), dtype=_x0.dtype)
    del _x0
    return _d

def reference(L0_attn_x, L0_attn_Wq, L0_attn_bq, L0_attn_Wk, L0_attn_bk, L0_attn_Wv, L0_attn_bv, L0_attn_Wo, L0_attn_bo, L0_ffn_gate_w, L0_ffn_up_w, L0_ffn_down_w, L0_ffn_gate_scale, L0_ffn_up_scale, L0_ffn_down_scale, L1_attn_wq, L1_attn_wk, L1_attn_wv, L1_attn_wo, L1_ffn_w_gate, L1_ffn_w_up, L1_ffn_w_down):

    def _L0_attn_ref(x, Wq, bq, Wk, bk, Wv, bv, Wo, bo):
        import jax, jax.numpy as jnp
        import numpy as np
        NUM_HEADS = 16
        NUM_KV_HEADS = 4
        ROPE_BASE = 10000.0

        def _rotate_half(x):
            x1 = x[..., ::2]
            x2 = x[..., 1::2]
            return jnp.stack((-x2, x1), axis=-1).reshape(x.shape)

        def apply_rope(x, positions, base):
            head_dim = x.shape[-1]
            inv_freq = 1.0 / base ** (jnp.arange(0, head_dim, 2, dtype=jnp.float32) / head_dim)
            freqs = positions.astype(jnp.float32)[:, None] * inv_freq[None, :]
            cos = jnp.repeat(jnp.cos(freqs), 2, axis=-1)[None, :, None, :]
            sin = jnp.repeat(jnp.sin(freqs), 2, axis=-1)[None, :, None, :]
            return x * cos + _rotate_half(x) * sin
        B, S, hidden = x.shape
        head_dim = hidden // NUM_HEADS
        scale = head_dim ** (-0.5)
        rep = NUM_HEADS // NUM_KV_HEADS
        positions = jnp.arange(S)
        q = (x @ Wq.T + bq).reshape(B, S, NUM_HEADS, head_dim)
        k = (x @ Wk.T + bk).reshape(B, S, NUM_KV_HEADS, head_dim)
        v = (x @ Wv.T + bv).reshape(B, S, NUM_KV_HEADS, head_dim)
        q = apply_rope(q, positions, ROPE_BASE)
        k = apply_rope(k, positions, ROPE_BASE)
        k = jnp.repeat(k, rep, axis=2)
        v = jnp.repeat(v, rep, axis=2)
        scores = jnp.einsum('bthd,bshd->bhts', q, k) * scale
        causal = jnp.tril(jnp.ones((S, S), dtype=bool))
        scores = jnp.where(causal[None, None, :, :], scores, -jnp.inf)
        probs = jax.nn.softmax(scores, axis=-1)
        attended = jnp.einsum('bhts,bshd->bthd', probs, v).reshape(B, S, hidden)
        return attended @ Wo.T + bo

    def _L0_ffn_ref(x, gate_w, up_w, down_w, gate_scale, up_scale, down_scale):
        import jax, jax.numpy as jnp
        import numpy as np
        B, S, H, I = (1, 64, 256, 768)

        def _quantized_matmul(x, w, scale):
            wq = w.astype(jnp.float8_e4m3fn).astype(x.dtype)
            y = jnp.einsum('bsi,io->bso', x, wq)
            return y * scale
        gate = jax.nn.silu(_quantized_matmul(x, gate_w, gate_scale))
        up = _quantized_matmul(x, up_w, up_scale)
        fuse = gate * up
        return _quantized_matmul(fuse, down_w, down_scale)

    def _L1_attn_ref(x, wq, wk, wv, wo):
        import jax, jax.numpy as jnp
        import numpy as np
        D_MODEL = 256
        N_HEADS = 16
        HEAD_DIM = D_MODEL // N_HEADS
        BATCH = 2
        SEQ = 256
        B, S, _ = x.shape

        def proj(w):
            return (x @ w.T).reshape(B, S, N_HEADS, HEAD_DIM).transpose(0, 2, 1, 3)
        q, k, v = (proj(wq), proj(wk), proj(wv))
        scale = 1.0 / np.sqrt(HEAD_DIM).astype(np.float32)
        scores = jnp.einsum('bhqd,bhkd->bhqk', q, k) * scale
        causal_mask = jnp.triu(jnp.ones((S, S), dtype=bool), k=1)
        scores = jnp.where(causal_mask, -jnp.inf, scores)
        attn = jax.nn.softmax(scores, axis=-1)
        out = jnp.einsum('bhqk,bhkd->bhqd', attn, v)
        out = out.transpose(0, 2, 1, 3).reshape(B, S, D_MODEL)
        return out @ wo.T

    def _L1_ffn_ref(x, w_gate, w_up, w_down):
        import jax, jax.numpy as jnp
        import numpy as np
        DIM_IN = 256
        DIM_HIDDEN = 1024
        gate = jnp.einsum('bsd,hd->bsh', x, w_gate)
        up = jnp.einsum('bsd,hd->bsh', x, w_up)
        gated = jax.nn.silu(gate) * up
        return jnp.einsum('bsh,dh->bsd', gated, w_down)
    x = L0_attn_x
    x = _layernorm(x + _L0_attn_ref(x, L0_attn_Wq, L0_attn_bq, L0_attn_Wk, L0_attn_bk, L0_attn_Wv, L0_attn_bv, L0_attn_Wo, L0_attn_bo), axis=-1)
    x = _layernorm(x + _L0_ffn_ref(x, L0_ffn_gate_w, L0_ffn_up_w, L0_ffn_down_w, L0_ffn_gate_scale, L0_ffn_up_scale, L0_ffn_down_scale), axis=-1)
    x = _layernorm(x + _L1_attn_ref(x, L1_attn_wq, L1_attn_wk, L1_attn_wv, L1_attn_wo), axis=-1)
    x = _layernorm(x + _L1_ffn_ref(x, L1_ffn_w_gate, L1_ffn_w_up, L1_ffn_w_down), axis=-1)
    return x

_drawn_inputs = setup_inputs


def setup_inputs(seed=0):
    import zlib

    import numpy as np

    out = dict(_drawn_inputs(seed))
    spreads = {'L0_attn_bq': (0.0, 0.8),
     'L0_attn_bk': (0.0, 0.8),
     'L0_attn_bv': (0.0, 0.1),
     'L0_attn_bo': (0.0, 0.1)}
    factors = {'L0_attn_Wq': 8.0,
     'L0_attn_Wk': 8.0,
     'L0_attn_Wv': 4.719,
     'L0_ffn_gate_scale': 5.239,
     'L0_ffn_up_scale': 6.054,
     'L0_ffn_down_scale': 5.883}
    for name, (base, spread) in spreads.items():
        noise = np.random.default_rng([zlib.crc32(name.encode()), seed]).standard_normal(out[name].shape)
        drawn = base * np.exp(spread * noise) if base else spread * noise
        out[name] = jnp.asarray(drawn.astype(out[name].dtype))
    for name, factor in factors.items():
        out[name] = (out[name] * factor).astype(out[name].dtype)
    return out
```

```python
import numpy as np
import concourse.bass as bass
from concourse import mybir
from contextlib import ExitStack


FP32 = mybir.dt.float32
BF16 = mybir.dt.bfloat16
INT32 = mybir.dt.int32
ACT = mybir.ActivationFunctionType
ALU = mybir.AluOpType
AX = mybir.AxisListType

P = 128
S = 2048
D = 256
DC = D // P
NT = S // P
TB = 4
NB = NT // TB
W = TB * P
HD = 16
HEADS = 16
HG = 4
NG = HEADS // HG
SCALE = HD ** -0.5
EPS = 1e-5
KVW = (HD, HG * HD)
KH = (1, HG)
QKV = (HEADS * HD + 2 * NG * HD, 3 * HEADS * HD)
KOFF = HEADS * HD
VOFF = (KOFF + NG * HD, 2 * KOFF)
ROPE = KOFF + NG * HD
FF = (768, 1024)
FC = (FF[0] // P, FF[1] // P)
SLOTS = NG + 1
KV_FILL = 16 * (1 + TB)
NEG = -1e30

QUADS = [(T, j, max(0, P * (j - TB * T))) for T in range(NB - 1, -1, -1)
         for j in list(range(TB * T, TB * T + TB)) + list(range(TB * T - 1, -1, -1))]
NQ = len(QUADS)
T_END = {T: max(q for q in range(NQ) if QUADS[q][0] == T) for T in range(NB)}
UNITS = [(c, i, h) for c in range(NB - 1, -1, -1) for T in range(NB - 1, c - 1, -1)
         for i in range(TB * T + TB - 1, TB * T - 1, -1) for h in range(HG)]
NU = len(UNITS)


def width(u):
    c, i, _ = UNITS[u]
    return min(W, P * (i + 1) - W * c)


CHUNK_END = {c: 1 + max(u for u in range(NU) if UNITS[u][0] == c) for c in range(NB)}
MAX_T_END = {T: 1 + max(u for u in range(NU) if UNITS[u][0] == 0 and UNITS[u][1] // TB == T) for T in range(NB)}


def unit_slots():
    out, u, cols, done = [], 0, 0, 0
    for q in range(NQ):
        for pair in range(2):
            cols += 2 * (W - QUADS[q][2])
            while u < NU - 4 and done + width(u) <= cols:
                done += width(u)
                u += 1
            out.append(u)
    return out


SLOT = unit_slots()
TURN_AT = {T_END[T] + 2: T for T in range(1, NB)}


def tidx(T):
    return NB - 1 - T


def network_kernel(nc, x, xT_d, wqkv_d, bqkv_d, wo_d, bo_d, gate_d, up_d, down_d,
                   gs_d, us_d, ds_d, rope_d, out):
    ctx = ExitStack()
    with ctx:
        def sb(name, shape, dt=FP32):
            return ctx.enter_context(nc.sbuf_tensor(name, shape, dt))

        def sem(name):
            return ctx.enter_context(nc.semaphore(name))

        X = sb("X", [P, NT, D])
        O = sb("O", [P, NT, D])
        xT = sb("xT", [P, DC, S])
        maxbuf = sb("maxbuf", [P, 2 * 4096])
        KT1 = maxbuf[:, 0:4096].bitcast(BF16).rearrange("p (T h w) -> p T h w", T=NB, h=HG)
        QT1 = maxbuf[:, 4096:8192].bitcast(BF16).rearrange("p (T h w) -> p T h w", T=NB, h=HG)
        spvbuf = sb("spvbuf", [P, 2 * 4096])
        KT2 = spvbuf[:, 0:4096].bitcast(BF16).rearrange("p (T h w) -> p T h w", T=NB, h=HG)
        QT2 = spvbuf[:, 4096:8192].bitcast(BF16).rearrange("p (T h w) -> p T h w", T=NB, h=HG)
        OcT = spvbuf[:, 0:4096].rearrange("p (c s) -> p c s", c=DC)
        KN = sb("KN", [P, NB, HG, TB, P], BF16)
        QN = sb("QN", [P, NB, HG, TB, P], BF16)
        PB = sb("PB", [P, 2, HG, W])
        VG = sb("VG", [P, NT, HG, 32])
        OT = sb("OT", [P, 2, W])
        wqkv = sb("wqkv", [P, DC, QKV[1]])
        wo = sb("wo", [P, DC, D])
        bqkv = sb("bqkv", [1, QKV[0]])
        bo = sb("bo", [1, D])
        ones_row = sb("ones_row", [1, P])
        rope = sb("rope", [P, NT, 2 * HD])
        row = spvbuf[:, 0:2 * QKV[1]].rearrange("p (r n) -> p r n", r=2)
        ra = spvbuf[:, 2048:2048 + 2 * ROPE].rearrange("p (r n) -> p r n", r=2)
        rb = spvbuf[:, 3072:3072 + 2 * ROPE].rearrange("p (r n) -> p r n", r=2)
        qs = sb("qs", [P, 2, TB, HG * HD])
        ks = sb("ks", [P, 2, TB, HG * HD])
        rq = sb("rq", [P, TB, HG * HD])
        rk = sb("rk", [P, TB, HG * HD])
        pm = sb("pm", [P, NB, TB, HG, NB])
        negm = sb("negm", [P, NB, TB, HG])
        rm = sb("rm", [P, TB, HG])
        rden = sb("rden", [P, TB, HG])
        stats = sb("stats", [P, NT, 6])
        mv = sb("mv", [P, NT, 2])
        rstd = sb("rstd", [P, NT])
        ident = sb("ident", [P, P])
        identb = sb("identb", [P, P], BF16)
        mask_qk = sb("mask_qk", [P, P], BF16)
        mask_kq = sb("mask_kq", [P, P], BF16)
        gs = sb("gs", [P, FC[0]])
        us = sb("us", [P, FC[0]])
        ds = sb("ds", [P, D])
        sl = sb("sl", [P, 2, W])
        yt = sb("yt", [P, 2, D])
        WG = [maxbuf[:, 0:DC * FF[L]].rearrange("p (c n) -> p c n", c=DC) for L in range(2)]
        WU = [maxbuf[:, 2048:2048 + DC * FF[L]].rearrange("p (c n) -> p c n", c=DC) for L in range(2)]
        WD = [maxbuf[:, 4096:4096 + FC[L] * D].rearrange("p (c n) -> p c n", c=FC[L]) for L in range(2)]
        tmpa = maxbuf[:, 6144:6144 + 768]
        tmpb = maxbuf[:, 6144 + 768:6144 + 2 * 768]
        hid = [PB[:, :, :, :].rearrange("p a h w -> p (a h) w"),
               spvbuf[:, 4096:8192].rearrange("p (n w) -> p n w", w=W)]

        ps = ctx.enter_context(nc.psum_tensor("ps", [P, 8, W], FP32))
        MXB, ACC, TRB = 4, 6, 7

        q_s = [nc.dram_tensor(f"q_s{L}", [SLOTS, S, HG * HD], FP32).ap() for L in range(2)]
        k_s = [nc.dram_tensor(f"k_s{L}", [SLOTS, S, KVW[L]], FP32).ap() for L in range(2)]
        v_s = [nc.dram_tensor(f"v_s{L}", [SLOTS, S, KVW[L]], FP32).ap() for L in range(2)]

        names = ("qkv_mm row_act row_dve max_ready max_read neg_max shift_step shift_done "
                 "prep_step prepk prepq s_ready exp_done pv_done ot_copied turned o_step o_norm "
                 "oT_ready oT_copied y_ready res_done stat_step stat_done sq_done rs_step ln_done "
                 "xT_ready xT_copied gu_ready silu_done hid_done down_ready "
                 "res2_done stat2_step stat2_done sq2_done rs2_step ln2_done").split()
        only0 = "rope_a rope_b y_scaled x2T_ready x2T_copied".split()

        sems = []
        for L in range(2):
            s = {n: sem(f"{n}{L}") for n in names + (only0 if L == 0 else [])}
            for kind in ("ak", "aq", "bk", "bq"):
                for T in range(NB):
                    s[kind, T] = sem(f"{kind}{T}_{L}")
            for kind in ("ldk", "ldq"):
                for r in range(2):
                    s[kind, r] = sem(f"{kind}{r}_{L}")
            s["scr"] = [sem(f"scr{r}_{L}") for r in range(2)]
            s["ffw"] = sem(f"ffw{L}")
            s["wload"] = sem(f"wload{L}")
            sems.append(s)
        x_in = sem("x_in")
        xT_in = [sem(f"xT_in{T}") for T in range(NB)]
        w_in = sem("w_in")
        b_in = sem("b_in")
        c_in = sem("c_in")
        const_step = sem("const_step")
        passed_sp = sem("passed_sp")
        passed_pool = sem("passed_pool")
        fill_step = sem("fill_step")
        quant_step = sem("quant_step")
        quant_done = sem("quant_done")
        out_done = sem("out_done")

        EXP_C, PV_C, OTC_C, TURN_C, NORM_C = 2, 2, 1, 2, 1

        def wait_count(eng, passed, sem_, value):
            eng.wait_ge(sem_, value)
            eng.sem_inc(passed, 1)

        block = ctx.enter_context(nc.Block())

        def sp_slices(sp, L, n, T):
            z = sems[L]
            sp.dma_start(ks[:, T % 2, :, 0:KVW[L]],
                         k_s[L][n, W * T:W * T + W, :].rearrange("(t p) c -> p t c", p=P)).then_inc(z["ldk", T % 2], 16)
            sp.dma_start(qs[:, T % 2, :, :],
                         q_s[L][n, W * T:W * T + W, :].rearrange("(t p) c -> p t c", p=P)).then_inc(z["ldq", T % 2], 16)

        def turn(sp, dst, src, T, heads):
            return sp.dma_start_transpose(
                dst[:, T, 0:heads, :].rearrange("p h (t w) -> p (h t) w", w=P),
                src[:, T, 0:heads, :, :].rearrange("p h t w -> p (h t w)"))

        def sp_max_keys(sp, L, n, T, prior):
            z = sems[L]
            wait_count(sp, passed_sp, z["prepk"], NB * n + tidx(T) + 1)
            if prior:
                wait_count(sp, passed_sp, z["max_ready"], NU * (n - 1) + CHUNK_END[T])
            turn(sp, KT1, KN, T, KH[L]).then_inc(z["ak", T], 16)

        def sp_max_queries(sp, L, n, T):
            z = sems[L]
            wait_count(sp, passed_sp, z["prepq"], NB * n + tidx(T) + 1)
            turn(sp, QT1, QN, T, HG).then_inc(z["aq", T], 16)

        def sp_spv_keys(sp, L, n, T, prior):
            z = sems[L]
            if prior:
                wait_count(sp, passed_sp, z["pv_done"], PV_C + NQ * (n - 1) + T_END[T] + 1)
            wait_count(sp, passed_sp, z["ak", T], 16 * (n + 1))
            turn(sp, KT2, KN, T, KH[L]).then_inc(z["bk", T], 16)
            for i in range(TB * T, TB * T + TB):
                sp.dma_start(VG[:, i, 0:KH[L], 0:HD],
                             v_s[L][n, P * i:P * i + P, :].rearrange("p (h d) -> p h d", d=HD))\
                    .then_inc(z["bk", T], 16)

        def sp_spv_queries(sp, L, n, T):
            z = sems[L]
            wait_count(sp, passed_sp, z["shift_done"], NB * n + tidx(T) + 1)
            turn(sp, QT2, QN, T, HG).then_inc(z["bq", T], 16)

        def sp_stage(sp, L, n, prior):
            z = sems[L]

            def slices(T):
                wait_count(sp, passed_sp, z["prepq"], NB * n + NB - 1 + tidx(T))
                sp_slices(sp, L, n + 1, T)

            for T in range(NB - 1, -1, -1):
                slices(T)
                if T == NB - 1:
                    sp_spv_keys(sp, L, n, T, prior)
                if T < NB - 1:
                    sp_max_queries(sp, L, n + 1, T + 1)
                sp_max_keys(sp, L, n + 1, T, True)
                sp_spv_queries(sp, L, n, T)
                if T > 0:
                    sp_spv_keys(sp, L, n, T - 1, prior)
            sp_max_queries(sp, L, n + 1, 0)

        def sp_last_fill(sp, L, n):
            for T in range(NB - 1, -1, -1):
                sp_spv_keys(sp, L, n, T, True)
                sp_spv_queries(sp, L, n, T)

        @block.sync
        def _(sp):
            for c in range(DC):
                sp.dma_start(wqkv[:, c, 0:QKV[0]], wqkv_d[0][c * P:c * P + P, :]).then_inc(w_in, 16)
            sp.dma_start(bqkv[:, :], bqkv_d[:, :]).then_inc(w_in, 16)
            for T in range(NB):
                for c in range(DC):
                    sp.dma_start(xT[:, c, W * T:W * T + W], xT_d[c * P:c * P + P, W * T:W * T + W])\
                        .then_inc(xT_in[T], 16)
                if T == 0:
                    sp.dma_start(rope[:, :, :], rope_d.rearrange("(t p) c -> p t c", p=P)).then_inc(c_in, 16)
            sp.dma_start(X[:, :, :], x.rearrange("(t p) c -> p t c", p=P)).then_inc(x_in, 16)
            sp.dma_start(bo[:, :], bo_d[:, :]).then_inc(b_in, 16)
            sp.dma_start(gs[:, :], gs_d[:, :]).then_inc(b_in, 16)
            sp.dma_start(us[:, :], us_d[:, :]).then_inc(b_in, 16)
            sp.dma_start(ds[:, :], ds_d[0:1, :].to_broadcast([P, D]))\
                .then_inc(b_in, 16)
            for L in range(2):
                z = sems[L]
                sp.dma_start(wo[:, :, :], wo_d[L].rearrange("(c p) n -> p c n", p=P)).then_inc(z["wload"], 16)
                for i in range(NT):
                    sp.wait_ge(z["row_act"], i + 1)
                    sp.wait_ge(z["row_dve"], i + 1)
                    r = i % 2
                    rows = slice(P * i, P * i + P)
                    for g0, g1, s0 in ((0, NG, 0), (NG, NG + 1, NG - 1)):
                        n = g1 - g0
                        sp.dma_start(q_s[L][g0:g1, rows, :].rearrange("g p c -> p g c"),
                                     row[:, r, s0 * HG * HD:(s0 + n) * HG * HD]
                                     .rearrange("p (g c) -> p g c", g=n)).then_inc(z["scr"][r], 16)
                        for dst, off in ((k_s[L], KOFF), (v_s[L], VOFF[L])):
                            sp.dma_start(dst[g0:g1, rows, :].rearrange("g p c -> p g c"),
                                         row[:, r, off + s0 * KVW[L]:off + (s0 + n) * KVW[L]]
                                         .rearrange("p (g c) -> p g c", g=n)).then_inc(z["scr"][r], 16)
                for r in range(2):
                    sp.wait_ge(z["scr"][r], 16 * 6 * NT // 2)
                if L == 0:
                    for c in range(DC):
                        sp.dma_start(wqkv[:, c, :], wqkv_d[1][c * P:c * P + P, :]).then_inc(sems[1]["wload"], 16)
                for T in range(NB - 1, -1, -1):
                    if T < NB - 2:
                        sp.wait_ge(z["prepq"], tidx(T) - 1)
                    sp_slices(sp, L, 0, T)
                for T in range(NB - 1, -1, -1):
                    sp_max_keys(sp, L, 0, T, False)
                    sp_max_queries(sp, L, 0, T)
                sp_stage(sp, L, 0, False)
                with sp.Fori(1, NG - 1) as n:
                    sp_stage(sp, L, n, True)
                sp_last_fill(sp, L, NG - 1)
                sp.wait_ge(z["max_ready"], NU * NG)
                sp.dma_start(WG[L], gate_d[L].rearrange("(c p) n -> p c n", p=P)).then_inc(z["ffw"], 16)
                sp.dma_start(WU[L], up_d[L].rearrange("(c p) n -> p c n", p=P)).then_inc(z["ffw"], 16)
                sp.dma_start(WD[L], down_d[L].rearrange("(c p) n -> p c n", p=P)).then_inc(z["ffw"], 16)
                if L == 0:
                    sp.wait_ge(z["y_ready"], NT // 2)
            for T in range(NB):
                sp.wait_ge(sems[1]["ln2_done"], TB * (T + 1))
                sp.dma_start(out[W * T:W * T + W, :].rearrange("(t p) c -> p t c", p=P),
                             X[:, TB * T:TB * T + TB, :]).then_inc(out_done, 16)
            sp.wait_ge(out_done, 16 * NB)

        def pool_split(pool, L, n, T, src, raw, dst, heads, parts, ld, done, step, prior, prior_count):
            z = sems[L]
            sp_, st = parts, step
            wait_count(pool, passed_pool, z[ld, T % 2], 16 * (2 * n + tidx(T) // 2 + 1))
            if prior:
                wait_count(pool, passed_pool, z[prior_count[0], T], prior_count[1] * n)


            def place(k):
                return dst[:, T, 0:heads, :, HD * k:HD * k + HD].rearrange("p h t d -> p t h d")

            f = src.rearrange("p t (h d) -> p t h d", d=HD)
            r = raw.rearrange("p t (h d) -> p t h d", d=HD)
            for k in sp_[0]:
                last = pool.tensor_copy(place(k), f)
            last.then_inc(z["prep_step"], 1)
            wait_count(pool, passed_pool, z["prep_step"], st)
            pool.tensor_tensor(r, f, place(sp_[0][0]), ALU.subtract).then_inc(z["prep_step"], 1)
            wait_count(pool, passed_pool, z["prep_step"], st + 1)
            for k in sp_[1]:
                last = pool.tensor_copy(place(k), r)
            last.then_inc(z["prep_step"], 1)
            wait_count(pool, passed_pool, z["prep_step"], st + 2)
            pool.tensor_tensor(place(sp_[2][0]), r, place(sp_[1][0]), ALU.subtract).then_inc(done, 1)

        KPARTS = ((0, 3, 5), (1, 4), (2,))
        QPARTS = ((0, 1, 2), (3, 4), (5,))
        PREP_STEPS = 6 * NB

        def pool_keys(pool, L, n, T, prior):
            pool_split(pool, L, n, T, ks[:, T % 2, :, 0:KVW[L]], rk[:, :, 0:KVW[L]], KN, KH[L], KPARTS, "ldk",
                       sems[L]["prepk"], PREP_STEPS * n + 6 * tidx(T) + 1, prior, ("bk", KV_FILL))

        def pool_queries(pool, L, n, T, prior):
            pool_split(pool, L, n, T, qs[:, T % 2, :, :], rq[:, :, :], QN, HG, QPARTS, "ldq",
                       sems[L]["prepq"], PREP_STEPS * n + 6 * tidx(T) + 4, prior, ("bq", 16))

        def pool_shift(pool, L, n, T):
            z = sems[L]
            wait_count(pool, passed_pool, z["neg_max"], NB * n + tidx(T) + 1)
            m = negm[:, T, :, :]

            def place(k):
                return QN[:, T, :, :, 6 * HD + k].rearrange("p h t -> p t h")

            st = 3 * (NB * n + tidx(T)) + 1
            pool.tensor_copy(place(0), m).then_inc(z["shift_step"], 1)
            wait_count(pool, passed_pool, z["shift_step"], st)
            pool.tensor_tensor(rm[:, :, :], m, place(0), ALU.subtract).then_inc(z["shift_step"], 1)
            wait_count(pool, passed_pool, z["shift_step"], st + 1)
            pool.tensor_copy(place(1), rm[:, :, :]).then_inc(z["shift_step"], 1)
            wait_count(pool, passed_pool, z["shift_step"], st + 2)
            pool.tensor_tensor(place(2), rm[:, :, :], place(1), ALU.subtract).then_inc(z["shift_done"], 1)

        def pool_stage(pool, L, n):
            for T in range(NB - 1, -1, -1):
                pool_keys(pool, L, n + 1, T, True)
                pool_shift(pool, L, n, T)
                pool_queries(pool, L, n + 1, T, True)

        @block.gpsimd
        def _(pool):
            pool.memset(ones_row[:, :], 1.0).then_inc(const_step, 1)
            pool.memset(ident[:, :], 0.0).then_inc(const_step, 1)
            pool.memset(mask_qk[:, :], 0.0).then_inc(const_step, 1)
            pool.memset(mask_kq[:, :], 0.0).then_inc(const_step, 1)
            pool.wait_ge(const_step, 4)
            pool.affine_select(out=ident[:, :], in_=ident[:, :], compare_op=ALU.not_equal, fill=1.0, base=0,
                               pattern=[[-1, P]], channel_multiplier=1).then_inc(const_step, 1)
            pool.affine_select(out=mask_qk[:, :], in_=mask_qk[:, :], compare_op=ALU.is_ge, fill=NEG, base=0,
                               pattern=[[-1, P]], channel_multiplier=1).then_inc(const_step, 1)
            pool.affine_select(out=mask_kq[:, :], in_=mask_kq[:, :], compare_op=ALU.is_ge, fill=NEG, base=0,
                               pattern=[[1, P]], channel_multiplier=-1).then_inc(const_step, 1)
            pool.wait_ge(const_step, 7)
            pool.tensor_copy(identb[:, :], ident[:, :]).then_inc(const_step, 1)
            pool.memset(QN[:, :, :, :, 6 * HD:P].rearrange("p T h t c -> p (T h t) c"), 0.0).then_inc(fill_step, 1)
            pool.memset(KN[:, :, :, :, 6 * HD:P].rearrange("p T h t c -> p (T h t) c"), 0.0).then_inc(fill_step, 1)
            pool.memset(VG[:, :, :, HD:32].rearrange("p t h c -> p (t h) c"), 0.0).then_inc(fill_step, 1)
            pool.wait_ge(fill_step, 3)
            pool.memset(KN[:, :, :, :, 6 * HD:6 * HD + 3].rearrange("p T h t c -> p (T h t) c"), 1.0)\
                .then_inc(fill_step, 1)
            pool.memset(VG[:, :, :, HD:HD + 1].rearrange("p t h c -> p (t h) c"), 1.0).then_inc(fill_step, 1)
            pool.wait_ge(fill_step, 5)
            for L in range(2):
                for T in range(NB - 1, -1, -1):
                    pool_keys(pool, L, 0, T, False)
                    pool_queries(pool, L, 0, T, False)
                pool_stage(pool, L, 0)
                with pool.Fori(1, NG - 1) as n:
                    pool_stage(pool, L, n)
                for T in range(NB - 1, -1, -1):
                    pool_shift(pool, L, NG - 1, T)

        def pe_unit(pe, L, n, u, first):
            z = sems[L]
            c, i, h = UNITS[u]
            w = width(u)
            if u == 0 or UNITS[u - 1][0] != c:
                pe.wait_ge(z["ak", c], 16 * (n + 1))
                pe.wait_ge(z["aq", c], 16 * (n + 1))
            if not (first and u < 2):
                pe.wait_ge(z["max_read"], NU * n + u - 1)
            bank = MXB + u % 2
            diag = W * c + w == P * (i + 1)
            hk = h if KH[L] > 1 else 0
            last = pe.matmul(ps[:, bank, 0:w], QT1[0:6 * HD, i // TB, h, P * (i % TB):P * (i % TB) + P],
                             KT1[0:6 * HD, c, hk, 0:w], start=True, stop=not diag)
            if diag:
                last = pe.matmul(ps[:, bank, w - P:w], identb[:, :], mask_qk[:, :], start=False, stop=True)
            last.then_inc(z["max_ready"], 1)

        def pe_scores(pe, L, g, q, pair):
            z = sems[L]
            T, j, off = QUADS[q]
            c = j // TB
            if pair == 0 and (q == 0 or QUADS[q - 1][0] != T):
                pe.wait_ge(z["bq", T], 16 * (g + 1))
            if pair == 0 and T == NB - 1 and (q == 0 or QUADS[q - 1][1] // TB != c):
                pe.wait_ge(z["bk", c], KV_FILL * (g + 1))
            pe.wait_ge(z["exp_done"], EXP_C + 2 * (NQ * g + q) + pair - 1)
            for h in (2 * pair, 2 * pair + 1):
                hk = h if KH[L] > 1 else 0
                diag = j >= TB * T
                last = pe.matmul(ps[:, h, off:W], KT2[:, c, hk, P * (j % TB):P * (j % TB) + P],
                                 QT2[:, T, h, off:W], start=True, stop=not diag)
                if diag:
                    last = pe.matmul(ps[:, h, off:off + P], identb[:, :], mask_kq[:, :], start=False, stop=True)
            last.then_inc(z["s_ready"], 1)

        def pe_pv(pe, L, g, q):
            z = sems[L]
            T, j, off = QUADS[q]
            first = j == TB * T
            if first:
                pe.wait_ge(z["ot_copied"], OTC_C + NB * g + tidx(T))
            pe.wait_ge(z["exp_done"], EXP_C + 2 * (NQ * g + q) + 2)
            for h in range(HG):
                hk = h if KH[L] > 1 else 0
                last = pe.matmul(ps[32 * h:32 * h + 32, ACC, off:W], VG[:, j, hk, :], PB[:, q % 2, h, off:W],
                                 start=first, stop=q == T_END[T])
            last.then_inc(z["pv_done"], 1)

        def pe_turn(pe, L, g, T):
            z = sems[L]
            pe.wait_ge(z["ot_copied"], OTC_C + NB * g + tidx(T) + 1)
            pe.wait_ge(z["o_norm"], NORM_C + NB * g + tidx(T))
            for t in range(TB):
                last = pe.transpose(ps[:, TRB, P * t:P * t + P], OT[:, T % 2, P * t:P * t + P], ident[:, :])
            last.then_inc(z["turned"], 1)

        def pe_stage(pe, L, g, with_max):
            u = 0
            for q in range(NQ):
                for pair in range(2):
                    pe_scores(pe, L, g, q, pair)
                    while with_max and u < SLOT[2 * q + pair]:
                        pe_unit(pe, L, g + 1, u, False)
                        u += 1
                if q > 0:
                    pe_pv(pe, L, g, q - 1)
                if q in TURN_AT:
                    pe_turn(pe, L, g, TURN_AT[q])
            pe_pv(pe, L, g, NQ - 1)
            while with_max and u < NU:
                pe_unit(pe, L, g + 1, u, False)
                u += 1
            pe_turn(pe, L, g, 0)

        def pe_rows(pe, L):
            z = sems[L]
            for i in range(NT):
                if L == 0 and i % TB == 0:
                    pe.wait_ge(xT_in[i // TB], 16 * DC)
                if L == 1 and i % TB == 0:
                    pe.wait_ge(sems[0]["x2T_copied"], 2 * (i // TB + 1))
                if i >= 2:
                    pe.wait_ge(z["row_act"], i - 1)
                    pe.wait_ge(z["row_dve"], i - 1)
                b = 2 * (i % 2)
                split = (ROPE, W)[L]
                parts = ((b, 0, split), (b + 1, split, QKV[L] - split))
                for bank, o, n in parts:
                    for c in range(DC):
                        last = pe.matmul(ps[:, bank, 0:n], xT[:, c, P * i:P * i + P], wqkv[:, c, o:o + n],
                                         start=c == 0, stop=L == 1 and c == DC - 1)
                    if L == 0:
                        last = pe.matmul(ps[:, bank, 0:n], ones_row[:, :], bqkv[:, o:o + n], start=False, stop=True)
                last.then_inc(z["qkv_mm"], 1)

        def pe_out(pe, L, T):
            z = sems[L]
            if T == 0:
                pe.wait_ge(z["wload"], 16 if L == 0 else 48)
                pe.wait_ge(z["o_norm"], NORM_C + NB * NG)
                if L == 0:
                    pe.wait_ge(b_in, 64)
            if T >= 1:
                pe.wait_ge(z["oT_copied"], 2 * T)
            for c in range(DC):
                for t in range(TB):
                    last = pe.transpose(ps[:, 4 + c, P * t:P * t + P], O[:, TB * T + t, P * c:P * c + P],
                                        ident[:, :])
                last.then_inc(z["oT_ready"], 1)
            pe.wait_ge(z["oT_copied"], 2 * (T + 1))
            for half in range(2):
                bank = 2 * (T % 2) + half
                if T >= 2:
                    pe.wait_ge(z["res_done"], TB * (T - 2) + 2 * half + 2)
                for t in (2 * half, 2 * half + 1):
                    i = TB * T + t
                    dst = ps[:, bank, D * (t % 2):D * (t % 2) + D]
                    for c in range(DC):
                        last = pe.matmul(dst, OcT[:, c, P * i:P * i + P], wo[:, c, :],
                                         start=c == 0, stop=L == 1 and c == DC - 1)
                    if L == 0:
                        last = pe.matmul(dst, ones_row[:, :], bo[:, :], start=False, stop=True)
                last.then_inc(z["y_ready"], 1)

        def pe_ffn_in(pe, L, T):
            z = sems[L]
            pe.wait_ge(z["ln_done"], TB * (T + 1))
            if T >= 1:
                pe.wait_ge(z["xT_copied"], 2 * T)
            else:
                pe.wait_ge(z["oT_copied"], 2 * NB)
            for c in range(DC):
                for t in range(TB):
                    last = pe.transpose(ps[:, 4 + c, P * t:P * t + P], X[:, TB * T + t, P * c:P * c + P],
                                        ident[:, :])
                last.then_inc(z["xT_ready"], 1)

        def pe_ffn(pe, L, T):
            z = sems[L]
            pe.wait_ge(z["xT_copied"], 2 * (T + 1))
            if T == 0:
                if L == 0:
                    pe.wait_ge(quant_done, 3)
                else:
                    pe.wait_ge(z["ffw"], 48)
                pe.wait_ge(z["res_done"], NT)
            for n in range(FC[L]):
                k = FC[L] * T + n
                b = 2 * (n % 2)
                if k >= 2:
                    pe.wait_ge(z["hid_done"], k - 1)
                for o, w in ((0, WG[L]), (1, WU[L])):
                    for c in range(DC):
                        last = pe.matmul(ps[:, b + o, :], w[:, c, P * n:P * n + P], xT[:, c, W * T:W * T + W],
                                         start=c == 0, stop=c == DC - 1)
                last.then_inc(z["gu_ready"], 1)
            if T + 1 < NB:
                pe_ffn_in(pe, L, T + 1)
            pe.wait_ge(z["hid_done"], FC[L] * (T + 1))
            for t in range(TB):
                if T >= 1:
                    pe.wait_ge(z["res2_done"], TB * (T - 1) + 2 * (t // 2) + 2)
                for n in range(FC[L]):
                    last = pe.matmul(ps[:, 6 + t // 2, D * (t % 2):D * (t % 2) + D],
                                     hid[T % 2][:, n, P * t:P * t + P], WD[L][:, n, :],
                                     start=n == 0, stop=n == FC[L] - 1)
                if t % 2:
                    last.then_inc(z["down_ready"], 1)

        def pe_next(pe, T):
            z = sems[0]
            pe.wait_ge(z["ln2_done"], TB * (T + 1))
            if T >= 1:
                pe.wait_ge(z["x2T_copied"], 2 * T)
            else:
                pe.wait_ge(z["xT_copied"], 2 * NB)
            for c in range(DC):
                for t in range(TB):
                    last = pe.transpose(ps[:, 4 + c, P * t:P * t + P], X[:, TB * T + t, P * c:P * c + P],
                                        ident[:, :])
                last.then_inc(z["x2T_ready"], 1)

        @block.tensor
        def _(pe):
            pe.wait_ge(const_step, 8)
            pe.wait_ge(w_in, 16 * (DC + 1))
            for L in range(2):
                z = sems[L]
                pe.sem_inc(z["pv_done"], PV_C)
                pe.sem_inc(z["turned"], TURN_C)
                if L == 1:
                    pe.wait_ge(z["wload"], 16 * DC)
                pe_rows(pe, L)
                for u in range(NU):
                    pe_unit(pe, L, 0, u, True)
                with pe.Fori(0, NG - 1) as g:
                    pe_stage(pe, L, g, True)
                pe_stage(pe, L, NG - 1, False)
                for T in range(NB):
                    pe_out(pe, L, T)
                pe_ffn_in(pe, L, 0)
                for T in range(NB):
                    pe_ffn(pe, L, T)
                if L == 0:
                    for T in range(NB):
                        pe_next(pe, T)

        def act_stage(act, L, g):
            z = sems[L]
            for q in range(NQ):
                T, j, off = QUADS[q]
                for pair in range(2):
                    act.wait_ge(z["s_ready"], 2 * (NQ * g + q) + pair + 1)
                    if pair == 0:
                        act.wait_ge(z["pv_done"], PV_C + NQ * g + q - 1)
                    act.activation(PB[:, q % 2, 2 * pair:2 * pair + 2, off:W], ps[:, 2 * pair:2 * pair + 2, off:W],
                                   ACT.Exp, scale=SCALE).then_inc(z["exp_done"], 1)
                done = [t for t in range(NB) if q == min(T_END[t] + 1, NQ - 1)]
                for t in done:
                    act.wait_ge(z["pv_done"], PV_C + NQ * g + T_END[t] + 1)
                    act.wait_ge(z["turned"], TURN_C + NB * g + tidx(t) - 1)
                    act.activation(OT[:, t % 2, :], ps[:, ACC, :], ACT.Copy).then_inc(z["ot_copied"], 1)

        @block.scalar
        def _(act):
            for L in range(2):
                z = sems[L]
                act.sem_inc(z["exp_done"], EXP_C)
                act.sem_inc(z["ot_copied"], OTC_C)
                for i in range(NT):
                    act.wait_ge(z["qkv_mm"], i + 1)
                    if i >= 2:
                        act.wait_ge(z["scr"][i % 2], 16 * 6 * (i // 2))
                    b = 2 * (i % 2)
                    if L == 0:
                        act.activation(row[:, i % 2, VOFF[0]:QKV[0]], ps[:, b + 1, 0:QKV[0] - VOFF[0]], ACT.Copy)\
                            .then_inc(z["row_act"], 1)
                    else:
                        act.activation(row[:, i % 2, W:QKV[1]], ps[:, b + 1, 0:QKV[1] - W], ACT.Copy)\
                            .then_inc(z["row_act"], 1)
                with act.Fori(0, NG) as g:
                    act_stage(act, L, g)
                for T in range(NB):
                    act.wait_ge(z["oT_ready"], 2 * T + 2)
                    act.activation(OcT[:, 1, W * T:W * T + W], ps[:, 5, :], ACT.Copy).then_inc(z["oT_copied"], 1)
                for T in range(NB):
                    act.wait_ge(z["stat_done"], T + 1)
                    act.activation(rstd[:, TB * T:TB * T + TB], rstd[:, TB * T:TB * T + TB], ACT.Sqrt)\
                        .then_inc(z["sq_done"], 1)
                for T in range(NB):
                    def x_copy(T):
                        act.wait_ge(z["xT_ready"], 2 * T + 2)
                        act.activation(xT[:, 1, W * T:W * T + W], ps[:, 5, :], ACT.Copy).then_inc(z["xT_copied"], 1)
                    if T == 0:
                        x_copy(0)
                    for n in range(FC[L]):
                        k = FC[L] * T + n
                        act.wait_ge(z["gu_ready"], k + 1)
                        if k >= 2:
                            act.wait_ge(z["hid_done"], k - 1)
                        act.activation(sl[:, n % 2, :], ps[:, 2 * (n % 2), :], ACT.Silu,
                                       scale=gs[:, n:n + 1] if L == 0 else 1.0).then_inc(z["silu_done"], 1)
                    if T + 1 < NB:
                        x_copy(T + 1)
                for T in range(NB):
                    act.wait_ge(z["stat2_done"], T + 1)
                    act.activation(rstd[:, TB * T:TB * T + TB], rstd[:, TB * T:TB * T + TB], ACT.Sqrt)\
                        .then_inc(z["sq2_done"], 1)
                if L == 0:
                    for T in range(NB):
                        act.wait_ge(z["x2T_ready"], 2 * T + 2)
                        act.activation(xT[:, 1, W * T:W * T + W], ps[:, 5, :], ACT.Copy)\
                            .then_inc(z["x2T_copied"], 1)

        def dve_unit(dve, L, n, u):
            z = sems[L]
            c, i, h = UNITS[u]
            dve.wait_ge(z["max_ready"], NU * n + u + 1)
            dve.tensor_reduce(pm[:, i // TB, i % TB, h, c:c + 1], ps[:, MXB + u % 2, 0:width(u)], AX.X, ALU.max)\
                .then_inc(z["max_read"], 1)

        def dve_neg_max(dve, L, n, T, first):
            z = sems[L]
            dve.wait_ge(z["max_read"], NU * n + MAX_T_END[T])
            if not first:
                dve.wait_ge(z["shift_done"], NB * (n - 1) + tidx(T) + 1)
            dve.tensor_reduce(negm[:, T, :, :], pm[:, T, :, :, 0:T + 1], AX.X, ALU.max, negate=True)\
                .then_inc(z["neg_max"], 1)

        def dve_units(dve, L, n, u, upto, first):
            while u < upto:
                dve_unit(dve, L, n, u)
                u += 1
                for T in range(NB):
                    if u == MAX_T_END[T]:
                        dve_neg_max(dve, L, n, T, first)
            return u

        def dve_norm(dve, L, g, T):
            z = sems[L]
            tr = ps[:, TRB, :].rearrange("p (t h c) -> p t h c", t=TB, h=HG)
            dve.wait_ge(z["turned"], TURN_C + NB * g + tidx(T) + 1)
            dve.reciprocal(rden[:, :, :], tr[:, :, :, HD]).then_inc(z["o_step"], 1)
            dve.wait_ge(z["o_step"], NB * g + tidx(T) + 1)
            dve.tensor_tensor(O[:, TB * T:TB * T + TB, bass.ds(g * (HG * HD), HG * HD)]
                              .rearrange("p t (h d) -> p t h d", d=HD), tr[:, :, :, 0:HD],
                              rden[:, :, :, None].to_broadcast([P, TB, HG, HD]), ALU.mult).then_inc(z["o_norm"], 1)

        def dve_stage(dve, L, g):
            u = 0
            for q in range(NQ):
                u = dve_units(dve, L, g + 1, u, SLOT[2 * q + 1], False)
                if q in TURN_AT:
                    dve_norm(dve, L, g, TURN_AT[q])
            dve_units(dve, L, g + 1, u, NU, False)
            dve_norm(dve, L, g, 0)

        def quantise(dve, w, n, st):
            a, b = tmpa[:, 0:n], tmpb[:, 0:n]

            def step(ins):
                st[0] += 1
                ins.then_inc(quant_step, 1)
                dve.wait_ge(quant_step, st[0])

            step(dve.tensor_scalar(a.bitcast(INT32), w.bitcast(INT32), 0x7F800000, None, ALU.bitwise_and))
            step(dve.tensor_scalar(a, a, 2.0 ** -6, 1.5 * 2.0 ** 20, ALU.max, ALU.mult))
            step(dve.tensor_tensor(b, w, a, ALU.add))
            step(dve.tensor_tensor(w, b, a, ALU.subtract))
            step(dve.tensor_tensor(b, w, w, ALU.mult))
            step(dve.tensor_scalar(a, b, 448.0 ** 2, 3.0e38, ALU.is_gt, ALU.mult))
            step(dve.tensor_tensor(b, a, a, ALU.mult))
            step(dve.tensor_tensor(b, b, b, ALU.subtract))
            step(dve.tensor_tensor(w, w, b, ALU.add))

        @block.vector
        def _(dve):
            for L in range(2):
                z = sems[L]
                dve.sem_inc(z["o_norm"], NORM_C)
                if L == 0:
                    dve.wait_ge(c_in, 16)
                for i in range(NT):
                    dve.wait_ge(z["qkv_mm"], i + 1)
                    if i >= 2:
                        dve.wait_ge(z["scr"][i % 2], 16 * 6 * (i // 2))
                    b = 2 * (i % 2)
                    r = i % 2
                    if L == 1:
                        dve.tensor_copy(row[:, r, 0:W], ps[:, b, :]).then_inc(z["row_dve"], 1)
                        continue
                    nh = ROPE // HD
                    src = ps[:, b, 0:ROPE].rearrange("p (h d) -> p h d", d=HD)
                    pairs = ps[:, b, 0:ROPE].rearrange("p (h d e) -> p h d e", d=HD // 2, e=2)
                    rbp = rb[:, r, :].rearrange("p (h d e) -> p h d e", d=HD // 2, e=2)
                    cos = rope[:, i, None, 0:HD].to_broadcast([P, nh, HD])
                    sn = rope[:, i, HD:2 * HD].rearrange("p (d e) -> p d e", e=2)
                    dve.tensor_tensor(ra[:, r, :].rearrange("p (h d) -> p h d", d=HD), src, cos, ALU.mult)\
                        .then_inc(z["rope_a"], 1)
                    for e in range(2):
                        dve.tensor_tensor(rbp[:, :, :, e], pairs[:, :, :, 1 - e],
                                          sn[:, None, :, e].to_broadcast([P, nh, HD // 2]), ALU.mult)\
                            .then_inc(z["rope_b"], 1)
                    dve.wait_ge(z["rope_a"], i + 1)
                    dve.wait_ge(z["rope_b"], 2 * (i + 1))
                    dve.tensor_tensor(row[:, r, 0:ROPE], ra[:, r, :], rb[:, r, :], ALU.add).then_inc(z["row_dve"], 1)
                dve_units(dve, L, 0, 0, NU, True)
                with dve.Fori(0, NG - 1) as g:
                    dve_stage(dve, L, g)
                if L == 0:
                    dve.wait_ge(z["ffw"], 48)
                    chunks = [w for buf, nn in ((WG[0], DC), (WU[0], DC)) for w in [buf[:, c, :] for c in range(nn)]]
                    dn = WD[0].rearrange("p c n -> p (c n)")
                    chunks += [dn[:, 0:768], dn[:, 768:1536]]
                st = [0]
                for T in range(NB - 1, -1, -1):
                    if L == 0:
                        for w in chunks[2 * tidx(T) - 2:2 * tidx(T)] if T < NB - 1 else ():
                            quantise(dve, w, 768, st)
                    dve_norm(dve, L, NG - 1, T)
                if L == 0:
                    dve.sem_inc(quant_done, 3)
                if L == 0:
                    dve.wait_ge(x_in, 16)
                for T in range(NB):
                    dve.wait_ge(z["oT_ready"], 2 * T + 1)
                    dve.tensor_copy(OcT[:, 0, W * T:W * T + W], ps[:, 4, :]).then_inc(z["oT_copied"], 1)
                    for t in range(TB):
                        i = TB * T + t
                        dve.wait_ge(z["y_ready"], 2 * T + t // 2 + 1)
                        y = ps[:, 2 * (T % 2) + t // 2, D * (t % 2):D * (t % 2) + D]
                        dve.tensor_tensor(X[:, i, :], y, X[:, i, :], ALU.add).then_inc(z["res_done"], 1)
                        dve.wait_ge(z["res_done"], i + 1)
                        dve.bn_stats(stats[:, i, :], X[:, i, :]).then_inc(z["stat_step"], 1)
                        dve.wait_ge(z["stat_step"], 2 * i + 1)
                        dve.bn_aggr(mv[:, i, :], stats[:, i, :]).then_inc(z["stat_step"], 1)
                    dve.wait_ge(z["stat_step"], 2 * TB * (T + 1))
                    dve.tensor_scalar(rstd[:, TB * T:TB * T + TB], mv[:, TB * T:TB * T + TB, 1], EPS, None, ALU.add)\
                        .then_inc(z["stat_done"], 1)
                for T in range(NB):
                    dve.wait_ge(z["sq_done"], T + 1)
                    dve.reciprocal(rstd[:, TB * T:TB * T + TB], rstd[:, TB * T:TB * T + TB]).then_inc(z["rs_step"], 1)
                    dve.wait_ge(z["rs_step"], T + 1)
                    for t in range(TB):
                        i = TB * T + t
                        dve.tensor_scalar(X[:, i, :], X[:, i, :], mv[:, i, 0:1], rstd[:, i:i + 1], ALU.subtract,
                                          ALU.mult).then_inc(z["ln_done"], 1)

                def x_copy(T):
                    dve.wait_ge(z["xT_ready"], 2 * T + 1)
                    dve.tensor_copy(xT[:, 0, W * T:W * T + W], ps[:, 4, :]).then_inc(z["xT_copied"], 1)

                x_copy(0)
                for T in range(NB):
                    for n in range(FC[L]):
                        k = FC[L] * T + n
                        if n == 0 and T >= 2:
                            dve.wait_ge(z["down_ready"], 2 * (T - 1))
                        dve.wait_ge(z["silu_done"], k + 1)
                        dve.wait_ge(z["gu_ready"], k + 1)
                        up = ps[:, 2 * (n % 2) + 1, :]
                        if L == 0:
                            dve.scalar_tensor_tensor(out=hid[T % 2][:, n, :], in0=up, scalar=us[:, n:n + 1],
                                                     in1=sl[:, n % 2, :], op0=ALU.mult, op1=ALU.mult)\
                                .then_inc(z["hid_done"], 1)
                        else:
                            dve.tensor_tensor(hid[T % 2][:, n, :], up, sl[:, n % 2, :], ALU.mult)\
                                .then_inc(z["hid_done"], 1)
                    if T + 1 < NB:
                        x_copy(T + 1)
                    for t in range(TB):
                        i = TB * T + t
                        if t % 2 == 0:
                            dve.wait_ge(z["down_ready"], 2 * T + t // 2 + 1)
                        y = ps[:, 6 + t // 2, D * (t % 2):D * (t % 2) + D]
                        if L == 0:
                            dve.tensor_tensor(yt[:, t % 2, :], y, ds[:, :], ALU.mult).then_inc(z["y_scaled"], 1)
                            dve.wait_ge(z["y_scaled"], i + 1)
                            y = yt[:, t % 2, :]
                        dve.tensor_tensor(X[:, i, :], y, X[:, i, :], ALU.add).then_inc(z["res2_done"], 1)
                        dve.wait_ge(z["res2_done"], i + 1)
                        dve.bn_stats(stats[:, i, :], X[:, i, :]).then_inc(z["stat2_step"], 1)
                        dve.wait_ge(z["stat2_step"], 2 * i + 1)
                        dve.bn_aggr(mv[:, i, :], stats[:, i, :]).then_inc(z["stat2_step"], 1)
                    dve.wait_ge(z["stat2_step"], 2 * TB * (T + 1))
                    dve.tensor_scalar(rstd[:, TB * T:TB * T + TB], mv[:, TB * T:TB * T + TB, 1], EPS, None, ALU.add)\
                        .then_inc(z["stat2_done"], 1)
                for T in range(NB):
                    dve.wait_ge(z["sq2_done"], T + 1)
                    dve.reciprocal(rstd[:, TB * T:TB * T + TB], rstd[:, TB * T:TB * T + TB]).then_inc(z["rs2_step"], 1)
                    dve.wait_ge(z["rs2_step"], T + 1)
                    for t in range(TB):
                        i = TB * T + t
                        dve.tensor_scalar(X[:, i, :], X[:, i, :], mv[:, i, 0:1], rstd[:, i:i + 1], ALU.subtract,
                                          ALU.mult).then_inc(z["ln2_done"], 1)
                if L == 0:
                    for T in range(NB):
                        dve.wait_ge(z["x2T_ready"], 2 * T + 1)
                        dve.tensor_copy(xT[:, 0, W * T:W * T + W], ps[:, 4, :]).then_inc(z["x2T_copied"], 1)


def _rope_table():
    inv_freq = np.float32(1.0) / np.power(np.float32(10000.0), np.arange(0, HD, 2, dtype=np.float32) / np.float32(HD))
    angle = np.arange(S, dtype=np.float32)[:, None] * inv_freq[None, :].astype(np.float32)
    cos, sin = np.cos(angle), np.sin(angle)
    return np.concatenate([np.repeat(cos, 2, axis=1), np.stack([-sin, sin], axis=-1).reshape(S, HD)],
                          axis=1).astype(np.float32)


def kernel(**inputs):
    import concourse.bacc as _bacc
    from concourse import mybir as _mybir
    from concourse.bass_utils import run_bass_kernel_spmd as _run

    i = inputs
    host = {
        "x": i["L0_attn_x"][0],
        "xT": i["L0_attn_x"][0].T,
        "wqkv0": np.concatenate([i["L0_attn_Wq"].T, i["L0_attn_Wk"].T, i["L0_attn_Wv"].T], axis=1),
        "wqkv1": np.concatenate([i["L1_attn_wq"].T, i["L1_attn_wk"].T, i["L1_attn_wv"].T], axis=1),
        "bqkv": np.concatenate([i["L0_attn_bq"], i["L0_attn_bk"], i["L0_attn_bv"]])[None, :],
        "wo0": i["L0_attn_Wo"].T,
        "wo1": i["L1_attn_wo"].T,
        "bo": i["L0_attn_bo"][None, :],
        "gate0": i["L0_ffn_gate_w"],
        "gate1": i["L1_ffn_w_gate"].T,
        "up0": i["L0_ffn_up_w"],
        "up1": i["L1_ffn_w_up"].T,
        "down0": i["L0_ffn_down_w"],
        "down1": i["L1_ffn_w_down"].T,
        "gs": i["L0_ffn_gate_scale"].reshape(FC[0], P).T,
        "us": i["L0_ffn_up_scale"].reshape(FC[0], P).T,
        "ds": i["L0_ffn_down_scale"][None, :],
        "rope": _rope_table(),
    }
    nc = _bacc.Bacc("TRN2", target_bir_lowering=False, num_devices=1)
    arrays, t = {}, {}
    for name, a in host.items():
        a = np.ascontiguousarray(a)
        arrays[f"in_{name}_dram"] = a
        t[name] = nc.dram_tensor(f"in_{name}_dram", a.shape, _mybir.dt.from_np(a.dtype), kind="ExternalInput").ap()
    out = nc.dram_tensor("out_0_dram", (1, S, D), FP32, kind="ExternalOutput").ap()
    network_kernel(nc, t["x"], t["xT"], (t["wqkv0"], t["wqkv1"]), t["bqkv"], (t["wo0"], t["wo1"]), t["bo"],
                   (t["gate0"], t["gate1"]), (t["up0"], t["up1"]), (t["down0"], t["down1"]), t["gs"], t["us"],
                   t["ds"], t["rope"], out[0])
    r = _run(nc, [arrays], core_ids=[0])
    return r.results[0]["out_0_dram"]
```

```python
import numpy as np
import concourse.bass as bass
from concourse import mybir
from contextlib import ExitStack


FP32 = mybir.dt.float32
BF16 = mybir.dt.bfloat16
INT32 = mybir.dt.int32
ACT = mybir.ActivationFunctionType
ALU = mybir.AluOpType
AX = mybir.AxisListType

P = 128
S = 2048
D = 256
DC = D // P
NT = S // P
TB = 4
NB = NT // TB
W = TB * P
HD = 16
HEADS = 16
HG = 4
NG = HEADS // HG
SCALE = HD ** -0.5
EPS = 1e-5
KVW = (HD, HG * HD)
KH = (1, HG)
QKV = (HEADS * HD + 2 * NG * HD, 3 * HEADS * HD)
KOFF = HEADS * HD
VOFF = (KOFF + NG * HD, 2 * KOFF)
ROPE = KOFF + NG * HD
FF = (768, 1024)
FC = (FF[0] // P, FF[1] // P)
NROW = 4
KV_FILL = 16 * (1 + TB)
NEG = -1e30

QUADS = [(T, j, max(0, P * (j - TB * T))) for T in range(NB) for j in range(TB * T + TB)]
NQ = len(QUADS)
T_END = [max(q for q in range(NQ) if QUADS[q][0] == T) for T in range(NB)]
KEYS_END = [max(q for q in range(NQ) if QUADS[q][1] // TB == c) for c in range(NB)]


def width(c, i):
    return min(W, P * (i + 1) - W * c)


def units_of(T):
    out = []
    for c in range(T + 1):
        for i in range(TB * T, TB * T + TB):
            n = max(1, W // width(c, i) if width(c, i) <= W // 2 else 1)
            out += [(c, i, tuple(range(h, h + n))) for h in range(0, HG, n)]
    return out


TOP = NB - 1
LOW = [u for T in range(TOP) for u in units_of(T)]
HIGH = units_of(TOP)
UNITS = HIGH + LOW
RING = (4, 5, 7)
TURN_AT = {T_END[T] + 2: T for T in range(TOP)}


def cols(u):
    return width(u[0], u[1]) * len(u[2])


def plan_stage(n_units):
    out, u, due, done = [], 0, 0, 0
    kept = 4 if n_units == len(UNITS) else 0

    def fill():
        nonlocal u, done
        while u < n_units - kept and done + cols(UNITS[u]) // 2 <= due:
            done += cols(UNITS[u])
            out.append(("unit", u))
            u += 1

    for q in range(NQ):
        for pair in range(2):
            out.append(("scores", q, pair))
            due += W - QUADS[q][2]
            fill()
        if q > 0:
            out.append(("pv", q - 1))
            due += 2 * (W - QUADS[q - 1][2])
            fill()
        if q in TURN_AT:
            out.append(("turn", TURN_AT[q]))
    out.append(("pv", NQ - 1))
    out += [("unit", k) for k in range(u, n_units)]
    out.append(("turn", TOP))
    return out


def entries_of(plan):
    return [x for x in plan if x[0] in ("unit", "turn")]


STAGE = plan_stage(len(UNITS))
LAST = plan_stage(len(HIGH))
ENTRIES = entries_of(STAGE)
NE = len(ENTRIES)
NLOW = len(LOW)
BASE_LAST = NLOW + NE * (NG - 1)
assert NE % len(RING) == 0


def entry_after(plan, what, k):
    return 1 + entries_of(plan).index((what, k))


FIRST = [("rows", T) for T in range(TOP)] + [("low", k) for k in range(len(units_of(0)))] + [("rows", TOP)] + \
        [("low", k) for k in range(len(units_of(0)), NLOW)]


def high_end(c):
    return entry_after(STAGE, "unit", max(k for k in range(len(HIGH)) if UNITS[k][0] == c))


def block_index(n, T):
    return NB * n + T


def network_kernel(nc, x, xT_d, wqkv_d, bqkv_d, wo_d, bo_d, gate_d, up_d, down_d,
                   gs_d, us_d, ds_d, rope_d, out):
    ctx = ExitStack()
    with ctx:
        def sb(name, shape, dt=FP32):
            return ctx.enter_context(nc.sbuf_tensor(name, shape, dt))

        def sem(name):
            return ctx.enter_context(nc.semaphore(name))

        X = sb("X", [P, NT, D])
        O = sb("O", [P, NT, D])
        xT = sb("xT", [P, DC, S])
        maxbuf = sb("maxbuf", [P, 2 * 4096])
        KT1 = maxbuf[:, 0:4096].bitcast(BF16).rearrange("p (T h w) -> p T h w", T=NB, h=HG)
        QT1 = maxbuf[:, 4096:8192].bitcast(BF16).rearrange("p (T h w) -> p T h w", T=NB, h=HG)
        spvbuf = sb("spvbuf", [P, 2 * 4096])
        KT2 = spvbuf[:, 0:4096].bitcast(BF16).rearrange("p (T h w) -> p T h w", T=NB, h=HG)
        QT2 = spvbuf[:, 4096:8192].bitcast(BF16).rearrange("p (T h w) -> p T h w", T=NB, h=HG)
        OcT = spvbuf[:, 0:4096].rearrange("p (c s) -> p c s", c=DC)
        KN = sb("KN", [P, NB, HG, TB, P], BF16)
        QN = sb("QN", [P, NB, HG, TB, P], BF16)
        PB = sb("PB", [P, 2, HG, W])
        pbf = PB[:, :, :, :].rearrange("p a h w -> p (a h w)")
        row = pbf[:, 0:NROW * QKV[1]].rearrange("p (r n) -> p r n", r=NROW)
        ra = pbf[:, NROW * QKV[1]:NROW * QKV[1] + ROPE]
        rb = pbf[:, NROW * QKV[1] + ROPE:NROW * QKV[1] + 2 * ROPE]
        VG = sb("VG", [P, NT, HG, 32])
        OT = sb("OT", [P, 2, W])
        wqkv = sb("wqkv", [P, DC, QKV[1]])
        wo = sb("wo", [P, DC, D])
        bqkv = sb("bqkv", [1, QKV[0]])
        bo = sb("bo", [1, D])
        ones_row = sb("ones_row", [1, P])
        rope = sb("rope", [P, NT, 2 * HD])
        qs = sb("qs", [P, 2, TB, HG * HD])
        ks = sb("ks", [P, 2, TB, HG * HD])
        rq = sb("rq", [P, TB, HG * HD])
        rk = sb("rk", [P, TB, HG * HD])
        pm = sb("pm", [P, NB, TB, HG, NB])
        negm = sb("negm", [P, NB, TB, HG])
        rm = sb("rm", [P, TB, HG])
        rden = sb("rden", [P, NB, TB, HG])
        stats = sb("stats", [P, NT, 6])
        mv = sb("mv", [P, NT, 2])
        rstd = sb("rstd", [P, NT])
        ident = sb("ident", [P, P])
        identb = sb("identb", [P, P], BF16)
        mask_qk = sb("mask_qk", [P, P], BF16)
        mask_kq = sb("mask_kq", [P, P], BF16)
        gs = sb("gs", [P, FC[0]])
        us = sb("us", [P, FC[0]])
        ds = sb("ds", [P, D])
        sl = sb("sl", [P, 2, W])
        yt = sb("yt", [P, 2, D])
        WG = [maxbuf[:, 0:DC * FF[L]].rearrange("p (c n) -> p c n", c=DC) for L in range(2)]
        WU = [maxbuf[:, 2048:2048 + DC * FF[L]].rearrange("p (c n) -> p c n", c=DC) for L in range(2)]
        WD = [maxbuf[:, 4096:4096 + FC[L] * D].rearrange("p (c n) -> p c n", c=FC[L]) for L in range(2)]
        tmpa = maxbuf[:, 6144:6144 + 768]
        tmpb = maxbuf[:, 6144 + 768:6144 + 2 * 768]
        hid = [PB[:, :, :, :].rearrange("p a h w -> p (a h) w"),
               spvbuf[:, 4096:8192].rearrange("p (n w) -> p n w", w=W)]

        ps = ctx.enter_context(nc.psum_tensor("ps", [P, 8, W], FP32))
        ACC = 6

        rows_s = [nc.dram_tensor(f"rows_s{L}", [S, QKV[L]], FP32).ap() for L in range(2)]

        names = ("qkv_mm row_act row_dve ring_ready ring_read neg_max shift_step shift_done "
                 "ldk_step ldq_step prepk prepq s_ready exp_done pv_done ot_copied o_step "
                 "oT_ready oT_copied y_ready res_done stat_step stat_done sq_done rs_step ln_done "
                 "xT_ready xT_copied gu_ready silu_done hid_done down_ready "
                 "res2_done stat2_step stat2_done sq2_done rs2_step ln2_done").split()
        only0 = "rope_a rope_b y_scaled x2T_ready x2T_copied".split()

        sems = []
        for L in range(2):
            s = {n: sem(f"{n}{L}") for n in names + (only0 if L == 0 else [])}
            for kind in ("ak", "aq", "bk", "bq"):
                for T in range(NB):
                    s[kind, T] = sem(f"{kind}{T}_{L}")
            for kind in ("ldk", "ldq"):
                for r in range(2):
                    s[kind, r] = sem(f"{kind}{r}_{L}")
            s["scr"] = [sem(f"scr{r}_{L}") for r in range(NROW)]
            s["ffw"] = sem(f"ffw{L}")
            s["wload"] = sem(f"wload{L}")
            sems.append(s)
        x_in = sem("x_in")
        xT_in = [sem(f"xT_in{T}") for T in range(NB)]
        w_in = sem("w_in")
        b_in = sem("b_in")
        c_in = sem("c_in")
        const_step = sem("const_step")
        passed_sp = sem("passed_sp")
        passed_pool = sem("passed_pool")
        fill_step = sem("fill_step")
        quant_step = sem("quant_step")
        quant_done = sem("quant_done")
        out_done = sem("out_done")

        EXP_C, PV_C, OTC_C = 2, 2, 1

        def wait_count(eng, passed, sem_, value):
            eng.wait_ge(sem_, value)
            eng.sem_inc(passed, 1)

        block = ctx.enter_context(nc.Block())

        def cols_of(L, T, first, n, w):
            return rows_s[L][W * T:W * T + W, bass.ds(n * w + first, w)]

        def sp_slices(sp, L, n, T):
            z = sems[L]
            r = T % 2
            if not (isinstance(n, int) and block_index(n, T) < 2):
                wait_count(sp, passed_sp, z["prepq"], block_index(n, T) - 1)
            sp.dma_start(ks[:, r, :, 0:KVW[L]],
                         cols_of(L, T, KOFF, n, KVW[L]).rearrange("(t p) c -> p t c", p=P)).then_inc(z["ldk", r], 16)
            sp.dma_start(qs[:, r, :, :],
                         cols_of(L, T, 0, n, HG * HD).rearrange("(t p) c -> p t c", p=P)).then_inc(z["ldq", r], 16)

        def turn(sp, dst, src, T, heads):
            return sp.dma_start_transpose(
                dst[:, T, 0:heads, :].rearrange("p h (t w) -> p (h t) w", w=P),
                src[:, T, 0:heads, :, :].rearrange("p h t w -> p (h t w)"))

        def sp_max_keys(sp, L, n, T, entries=None):
            z = sems[L]
            wait_count(sp, passed_sp, z["prepk"], block_index(n, T) + 1)
            if entries is not None:
                wait_count(sp, passed_sp, z["ring_ready"], entries)
            turn(sp, KT1, KN, T, KH[L]).then_inc(z["ak", T], 16)

        def sp_max_queries(sp, L, n, T):
            z = sems[L]
            wait_count(sp, passed_sp, z["prepq"], block_index(n, T) + 1)
            turn(sp, QT1, QN, T, HG).then_inc(z["aq", T], 16)

        def sp_spv_keys(sp, L, n, T, quads=None):
            z = sems[L]
            if quads is not None:
                wait_count(sp, passed_sp, z["pv_done"], PV_C + quads)
            wait_count(sp, passed_sp, z["ak", T], 16 * (n + 1))
            turn(sp, KT2, KN, T, KH[L]).then_inc(z["bk", T], 16)
            for i in range(TB * T, TB * T + TB):
                sp.dma_start(VG[:, i, 0:KH[L], 0:HD],
                             rows_s[L][P * i:P * i + P, bass.ds(n * KVW[L] + VOFF[L], KVW[L])].rearrange("p (h d) -> p h d", d=HD))\
                    .then_inc(z["bk", T], 16)

        def sp_spv_queries(sp, L, n, T, quads=None):
            z = sems[L]
            if quads is not None:
                wait_count(sp, passed_sp, z["pv_done"], PV_C + quads)
            wait_count(sp, passed_sp, z["shift_done"], block_index(n, T) + 1)
            turn(sp, QT2, QN, T, HG).then_inc(z["bq", T], 16)

        def sp_stage(sp, L, g):
            m = g + 1

            def keys(T):
                sp_max_keys(sp, L, m, T, NLOW + NE * g + high_end(T))

            sp_slices(sp, L, m, 0)
            sp_slices(sp, L, m, 1)
            sp_slices(sp, L, m, 2)
            for T in range(2):
                keys(T)
                sp_max_queries(sp, L, m, T)
            keys(2)
            sp_spv_queries(sp, L, g, TOP, NQ * g)
            sp_slices(sp, L, m, TOP)
            sp_max_queries(sp, L, m, 2)
            keys(TOP)
            sp_max_queries(sp, L, m, TOP)
            for T in range(2):
                sp_spv_queries(sp, L, m, T, NQ * g + T_END[T] + 1)
            for T in range(NB):
                sp_spv_keys(sp, L, m, T, NQ * g + KEYS_END[T] + 1)
                if T == 2:
                    sp_spv_queries(sp, L, m, T, NQ * g + T_END[T] + 1)

        def sp_rows_stored(sp, L, T):
            for r in range(NROW):
                sp.wait_ge(sems[L]["scr"][r], 16 * (T + 1))

        @block.sync
        def _(sp):
            for c in range(DC):
                sp.dma_start(wqkv[:, c, 0:QKV[0]], wqkv_d[0][c * P:c * P + P, :]).then_inc(w_in, 16)
            sp.dma_start(bqkv[:, :], bqkv_d[:, :]).then_inc(w_in, 16)
            for T in range(NB):
                for c in range(DC):
                    sp.dma_start(xT[:, c, W * T:W * T + W], xT_d[c * P:c * P + P, W * T:W * T + W])\
                        .then_inc(xT_in[T], 16)
                if T == 0:
                    sp.dma_start(rope[:, :, :], rope_d.rearrange("(t p) c -> p t c", p=P)).then_inc(c_in, 16)
            sp.dma_start(X[:, :, :], x.rearrange("(t p) c -> p t c", p=P)).then_inc(x_in, 16)
            sp.dma_start(bo[:, :], bo_d[:, :]).then_inc(b_in, 16)
            sp.dma_start(gs[:, :], gs_d[:, :]).then_inc(b_in, 16)
            sp.dma_start(us[:, :], us_d[:, :]).then_inc(b_in, 16)
            sp.dma_start(ds[:, :], ds_d[0:1, :].to_broadcast([P, D]))\
                .then_inc(b_in, 16)
            for L in range(2):
                z = sems[L]
                sp.dma_start(wo[:, :, :], wo_d[L].rearrange("(c p) n -> p c n", p=P)).then_inc(z["wload"], 16)
                for T in range(NB):
                    sp_rows_stored(sp, L, T)
                    sp_slices(sp, L, 0, T)
                    sp_max_keys(sp, L, 0, T)
                    sp_max_queries(sp, L, 0, T)
                    sp_spv_keys(sp, L, 0, T)
                if L == 0:
                    for c in range(DC):
                        sp.dma_start(wqkv[:, c, :], wqkv_d[1][c * P:c * P + P, :]).then_inc(sems[1]["wload"], 16)
                for T in range(TOP):
                    sp_spv_queries(sp, L, 0, T)
                with sp.Fori(0, NG - 1) as g:
                    sp_stage(sp, L, g)
                sp_spv_queries(sp, L, NG - 1, TOP, NQ * (NG - 1))
                sp.wait_ge(z["ring_ready"], BASE_LAST + entry_after(LAST, "unit", len(HIGH) - 1))
                sp.dma_start(WG[L], gate_d[L].rearrange("(c p) n -> p c n", p=P)).then_inc(z["ffw"], 16)
                sp.dma_start(WU[L], up_d[L].rearrange("(c p) n -> p c n", p=P)).then_inc(z["ffw"], 16)
                sp.dma_start(WD[L], down_d[L].rearrange("(c p) n -> p c n", p=P)).then_inc(z["ffw"], 16)
                if L == 0:
                    sp.wait_ge(z["y_ready"], NT // 2)
            for T in range(NB):
                sp.wait_ge(sems[1]["ln2_done"], TB * (T + 1))
                sp.dma_start(out[W * T:W * T + W, :].rearrange("(t p) c -> p t c", p=P),
                             X[:, TB * T:TB * T + TB, :]).then_inc(out_done, 16)
            sp.wait_ge(out_done, 16 * NB)

        def pool_split(pool, L, n, T, src, raw, dst, heads, parts, ld, done, step, prior_count):
            z = sems[L]
            sp_, st = parts, step
            wait_count(pool, passed_pool, z[ld, T % 2], 16 * (NB // 2 * n + T // 2 + 1))
            if not (isinstance(n, int) and n == 0):
                wait_count(pool, passed_pool, z[prior_count[0], T], prior_count[1] * n)


            def place(k):
                return dst[:, T, 0:heads, :, HD * k:HD * k + HD].rearrange("p h t d -> p t h d")

            f = src.rearrange("p t (h d) -> p t h d", d=HD)
            r = raw.rearrange("p t (h d) -> p t h d", d=HD)
            for k in sp_[0]:
                last = pool.tensor_copy(place(k), f)
            last.then_inc(z[ld + "_step"], 1)
            wait_count(pool, passed_pool, z[ld + "_step"], st)
            pool.tensor_tensor(r, f, place(sp_[0][0]), ALU.subtract).then_inc(z[ld + "_step"], 1)
            wait_count(pool, passed_pool, z[ld + "_step"], st + 1)
            for k in sp_[1]:
                last = pool.tensor_copy(place(k), r)
            last.then_inc(z[ld + "_step"], 1)
            wait_count(pool, passed_pool, z[ld + "_step"], st + 2)
            pool.tensor_tensor(place(sp_[2][0]), r, place(sp_[1][0]), ALU.subtract).then_inc(done, 1)

        KPARTS = ((0, 3, 5), (1, 4), (2,))
        QPARTS = ((0, 1, 2), (3, 4), (5,))

        def pool_keys(pool, L, n, T):
            pool_split(pool, L, n, T, ks[:, T % 2, :, 0:KVW[L]], rk[:, :, 0:KVW[L]], KN, KH[L], KPARTS,
                       "ldk", sems[L]["prepk"], 3 * block_index(n, T) + 1, ("bk", KV_FILL))

        def pool_queries(pool, L, n, T):
            pool_split(pool, L, n, T, qs[:, T % 2, :, :], rq[:, :, :], QN, HG, QPARTS,
                       "ldq", sems[L]["prepq"], 3 * block_index(n, T) + 1, ("bq", 16))

        def pool_shift(pool, L, n, T):
            z = sems[L]
            wait_count(pool, passed_pool, z["neg_max"], block_index(n, T) + 1)
            m = negm[:, T, :, :]

            def place(k):
                return QN[:, T, :, :, 6 * HD + k].rearrange("p h t -> p t h")

            st = 3 * block_index(n, T) + 1
            pool.tensor_copy(place(0), m).then_inc(z["shift_step"], 1)
            wait_count(pool, passed_pool, z["shift_step"], st)
            pool.tensor_tensor(rm[:, :, :], m, place(0), ALU.subtract).then_inc(z["shift_step"], 1)
            wait_count(pool, passed_pool, z["shift_step"], st + 1)
            pool.tensor_copy(place(1), rm[:, :, :]).then_inc(z["shift_step"], 1)
            wait_count(pool, passed_pool, z["shift_step"], st + 2)
            pool.tensor_tensor(place(2), rm[:, :, :], place(1), ALU.subtract).then_inc(z["shift_done"], 1)

        def pool_stage(pool, L, g):
            for T in range(2):
                pool_keys(pool, L, g + 1, T)
                pool_queries(pool, L, g + 1, T)
            pool_keys(pool, L, g + 1, 2)
            pool_shift(pool, L, g, TOP)
            pool_queries(pool, L, g + 1, 2)
            pool_keys(pool, L, g + 1, TOP)
            pool_queries(pool, L, g + 1, TOP)
            for T in range(TOP):
                pool_shift(pool, L, g + 1, T)

        @block.gpsimd
        def _(pool):
            pool.memset(ones_row[:, :], 1.0).then_inc(const_step, 1)
            pool.memset(ident[:, :], 0.0).then_inc(const_step, 1)
            pool.memset(mask_qk[:, :], 0.0).then_inc(const_step, 1)
            pool.memset(mask_kq[:, :], 0.0).then_inc(const_step, 1)
            pool.wait_ge(const_step, 4)
            pool.affine_select(out=ident[:, :], in_=ident[:, :], compare_op=ALU.not_equal, fill=1.0, base=0,
                               pattern=[[-1, P]], channel_multiplier=1).then_inc(const_step, 1)
            pool.affine_select(out=mask_qk[:, :], in_=mask_qk[:, :], compare_op=ALU.is_ge, fill=NEG, base=0,
                               pattern=[[-1, P]], channel_multiplier=1).then_inc(const_step, 1)
            pool.affine_select(out=mask_kq[:, :], in_=mask_kq[:, :], compare_op=ALU.is_ge, fill=NEG, base=0,
                               pattern=[[1, P]], channel_multiplier=-1).then_inc(const_step, 1)
            pool.wait_ge(const_step, 7)
            pool.tensor_copy(identb[:, :], ident[:, :]).then_inc(const_step, 1)
            pool.memset(QN[:, :, :, :, 6 * HD:P].rearrange("p T h t c -> p (T h t) c"), 0.0).then_inc(fill_step, 1)
            pool.memset(KN[:, :, :, :, 6 * HD:P].rearrange("p T h t c -> p (T h t) c"), 0.0).then_inc(fill_step, 1)
            pool.memset(VG[:, :, :, HD:32].rearrange("p t h c -> p (t h) c"), 0.0).then_inc(fill_step, 1)
            pool.wait_ge(fill_step, 3)
            pool.memset(KN[:, :, :, :, 6 * HD:6 * HD + 3].rearrange("p T h t c -> p (T h t) c"), 1.0)\
                .then_inc(fill_step, 1)
            pool.memset(VG[:, :, :, HD:HD + 1].rearrange("p t h c -> p (t h) c"), 1.0).then_inc(fill_step, 1)
            pool.wait_ge(fill_step, 5)
            for L in range(2):
                for T in range(TOP):
                    pool_keys(pool, L, 0, T)
                    pool_queries(pool, L, 0, T)
                pool_shift(pool, L, 0, 0)
                pool_shift(pool, L, 0, 1)
                pool_keys(pool, L, 0, TOP)
                pool_queries(pool, L, 0, TOP)
                pool_shift(pool, L, 0, 2)
                with pool.Fori(0, NG - 1) as g:
                    pool_stage(pool, L, g)
                pool_shift(pool, L, NG - 1, TOP)

        def pe_ring(pe, L, e):
            if not (isinstance(e, int) and e < len(RING)):
                pe.wait_ge(sems[L]["ring_read"], e - len(RING) + 1)

        def pe_unit(pe, L, n, unit, before, e, bank):
            z = sems[L]
            c, i, heads = unit
            w = width(c, i)
            fresh = before is None or before[1] // TB != i // TB
            if fresh or before[0] != c:
                pe.wait_ge(z["ak", c], 16 * (n + 1))
            if fresh:
                pe.wait_ge(z["aq", i // TB], 16 * (n + 1))
            pe_ring(pe, L, e)
            diag = W * c + w == P * (i + 1)
            for k, h in enumerate(heads):
                hk = h if KH[L] > 1 else 0
                o = w * k
                last = pe.matmul(ps[:, bank, o:o + w], QT1[0:6 * HD, i // TB, h, P * (i % TB):P * (i % TB) + P],
                                 KT1[0:6 * HD, c, hk, 0:w], start=True, stop=not diag)
                if diag:
                    last = pe.matmul(ps[:, bank, o + w - P:o + w], identb[:, :], mask_qk[:, :],
                                     start=False, stop=True)
            last.then_inc(z["ring_ready"], 1)

        def pe_scores(pe, L, g, q, pair):
            z = sems[L]
            T, j, off = QUADS[q]
            c = j // TB
            if pair == 0 and j == 0:
                pe.wait_ge(z["bq", T], 16 * (g + 1))
            if pair == 0 and T == c and j == TB * c:
                pe.wait_ge(z["bk", c], KV_FILL * (g + 1))
            pe.wait_ge(z["exp_done"], EXP_C + 2 * (NQ * g + q) + pair - 1)
            for h in (2 * pair, 2 * pair + 1):
                hk = h if KH[L] > 1 else 0
                diag = j >= TB * T
                last = pe.matmul(ps[:, h, off:W], KT2[:, c, hk, P * (j % TB):P * (j % TB) + P],
                                 QT2[:, T, h, off:W], start=True, stop=not diag)
                if diag:
                    last = pe.matmul(ps[:, h, off:off + P], identb[:, :], mask_kq[:, :], start=False, stop=True)
            last.then_inc(z["s_ready"], 1)

        def pe_pv(pe, L, g, q):
            z = sems[L]
            T, j, off = QUADS[q]
            first = j == 0
            if first:
                pe.wait_ge(z["ot_copied"], OTC_C + NB * g + T)
            pe.wait_ge(z["exp_done"], EXP_C + 2 * (NQ * g + q) + 2)
            for h in range(HG):
                hk = h if KH[L] > 1 else 0
                last = pe.matmul(ps[32 * h:32 * h + 32, ACC, off:W], VG[:, j, hk, :], PB[:, q % 2, h, off:W],
                                 start=first, stop=q == T_END[T])
            last.then_inc(z["pv_done"], 1)

        def pe_turn(pe, L, g, T, e, bank):
            z = sems[L]
            pe.wait_ge(z["ot_copied"], OTC_C + NB * g + T + 1)
            pe_ring(pe, L, e)
            for t in range(TB):
                last = pe.transpose(ps[:, bank, P * t:P * t + P], OT[:, T % 2, P * t:P * t + P], ident[:, :])
            last.then_inc(z["ring_ready"], 1)

        def pe_stage(pe, L, g, plan, base):
            e = 0
            before = None
            for what, k, *pair in plan:
                if what == "scores":
                    pe_scores(pe, L, g, k, pair[0])
                elif what == "pv":
                    pe_pv(pe, L, g, k)
                else:
                    bank = RING[(NLOW + e) % len(RING)]
                    if what == "unit":
                        pe_unit(pe, L, g if k < len(HIGH) else g + 1, UNITS[k], before, base + e, bank)
                        before = UNITS[k]
                    else:
                        pe_turn(pe, L, g, k, base + e, bank)
                    e += 1

        def pe_rows(pe, L, T):
            z = sems[L]
            for i in range(TB * T, TB * T + TB):
                if L == 0 and i % TB == 0:
                    pe.wait_ge(xT_in[i // TB], 16 * DC)
                if L == 1 and i % TB == 0:
                    pe.wait_ge(sems[0]["x2T_copied"], 2 * (i // TB + 1))
                if i >= 2:
                    pe.wait_ge(z["row_act"], i - 1)
                    pe.wait_ge(z["row_dve"], i - 1)
                b = 2 * (i % 2)
                split = (ROPE, W)[L]
                parts = ((b, 0, split), (b + 1, split, QKV[L] - split))
                for bank, o, n in parts:
                    for c in range(DC):
                        last = pe.matmul(ps[:, bank, 0:n], xT[:, c, P * i:P * i + P], wqkv[:, c, o:o + n],
                                         start=c == 0, stop=L == 1 and c == DC - 1)
                    if L == 0:
                        last = pe.matmul(ps[:, bank, 0:n], ones_row[:, :], bqkv[:, o:o + n], start=False, stop=True)
                last.then_inc(z["qkv_mm"], 1)

        def pe_out(pe, L, T):
            z = sems[L]
            if T == 0:
                pe.wait_ge(z["wload"], 16 if L == 0 else 48)
                pe.wait_ge(z["ring_read"], BASE_LAST + len(entries_of(LAST)))
                if L == 0:
                    pe.wait_ge(b_in, 64)
            if T >= 1:
                pe.wait_ge(z["oT_copied"], 2 * T)
            for c in range(DC):
                for t in range(TB):
                    last = pe.transpose(ps[:, 4 + c, P * t:P * t + P], O[:, TB * T + t, P * c:P * c + P],
                                        ident[:, :])
                last.then_inc(z["oT_ready"], 1)
            pe.wait_ge(z["oT_copied"], 2 * (T + 1))
            for half in range(2):
                bank = 2 * (T % 2) + half
                if T >= 2:
                    pe.wait_ge(z["res_done"], TB * (T - 2) + 2 * half + 2)
                for t in (2 * half, 2 * half + 1):
                    i = TB * T + t
                    dst = ps[:, bank, D * (t % 2):D * (t % 2) + D]
                    for c in range(DC):
                        last = pe.matmul(dst, OcT[:, c, P * i:P * i + P], wo[:, c, :],
                                         start=c == 0, stop=L == 1 and c == DC - 1)
                    if L == 0:
                        last = pe.matmul(dst, ones_row[:, :], bo[:, :], start=False, stop=True)
                last.then_inc(z["y_ready"], 1)

        def pe_ffn_in(pe, L, T):
            z = sems[L]
            pe.wait_ge(z["ln_done"], TB * (T + 1))
            if T >= 1:
                pe.wait_ge(z["xT_copied"], 2 * T)
            else:
                pe.wait_ge(z["oT_copied"], 2 * NB)
            for c in range(DC):
                for t in range(TB):
                    last = pe.transpose(ps[:, 4 + c, P * t:P * t + P], X[:, TB * T + t, P * c:P * c + P],
                                        ident[:, :])
                last.then_inc(z["xT_ready"], 1)

        def pe_ffn(pe, L, T):
            z = sems[L]
            pe.wait_ge(z["xT_copied"], 2 * (T + 1))
            if T == 0:
                if L == 0:
                    pe.wait_ge(quant_done, 3)
                else:
                    pe.wait_ge(z["ffw"], 48)
                pe.wait_ge(z["res_done"], NT)
            for n in range(FC[L]):
                k = FC[L] * T + n
                b = 2 * (n % 2)
                if k >= 2:
                    pe.wait_ge(z["hid_done"], k - 1)
                for o, w in ((0, WG[L]), (1, WU[L])):
                    for c in range(DC):
                        last = pe.matmul(ps[:, b + o, :], w[:, c, P * n:P * n + P], xT[:, c, W * T:W * T + W],
                                         start=c == 0, stop=c == DC - 1)
                last.then_inc(z["gu_ready"], 1)
            if T + 1 < NB:
                pe_ffn_in(pe, L, T + 1)
            pe.wait_ge(z["hid_done"], FC[L] * (T + 1))
            for t in range(TB):
                if T >= 1:
                    pe.wait_ge(z["res2_done"], TB * (T - 1) + 2 * (t // 2) + 2)
                for n in range(FC[L]):
                    last = pe.matmul(ps[:, 6 + t // 2, D * (t % 2):D * (t % 2) + D],
                                     hid[T % 2][:, n, P * t:P * t + P], WD[L][:, n, :],
                                     start=n == 0, stop=n == FC[L] - 1)
                if t % 2:
                    last.then_inc(z["down_ready"], 1)

        def pe_next(pe, T):
            z = sems[0]
            pe.wait_ge(z["ln2_done"], TB * (T + 1))
            if T >= 1:
                pe.wait_ge(z["x2T_copied"], 2 * T)
            else:
                pe.wait_ge(z["xT_copied"], 2 * NB)
            for c in range(DC):
                for t in range(TB):
                    last = pe.transpose(ps[:, 4 + c, P * t:P * t + P], X[:, TB * T + t, P * c:P * c + P],
                                        ident[:, :])
                last.then_inc(z["x2T_ready"], 1)

        @block.tensor
        def _(pe):
            pe.wait_ge(const_step, 8)
            pe.wait_ge(w_in, 16 * (DC + 1))
            for L in range(2):
                z = sems[L]
                pe.sem_inc(z["pv_done"], PV_C)
                if L == 1:
                    pe.wait_ge(z["wload"], 16 * DC)
                for what, k in FIRST:
                    if what == "rows":
                        pe_rows(pe, L, k)
                    else:
                        pe_unit(pe, L, 0, LOW[k], LOW[k - 1] if k else None, k, RING[k % len(RING)])
                with pe.Fori(0, NG - 1) as g:
                    pe_stage(pe, L, g, STAGE, NLOW + NE * g)
                pe_stage(pe, L, NG - 1, LAST, BASE_LAST)
                for T in range(NB):
                    pe_out(pe, L, T)
                pe_ffn_in(pe, L, 0)
                for T in range(NB):
                    pe_ffn(pe, L, T)
                if L == 0:
                    for T in range(NB):
                        pe_next(pe, T)

        def act_stage(act, L, g, plan, base):
            z = sems[L]
            for q in range(NQ):
                T, j, off = QUADS[q]
                for pair in range(2):
                    act.wait_ge(z["s_ready"], 2 * (NQ * g + q) + pair + 1)
                    if pair == 0:
                        act.wait_ge(z["pv_done"], PV_C + NQ * g + q - 1)
                    act.activation(PB[:, q % 2, 2 * pair:2 * pair + 2, off:W], ps[:, 2 * pair:2 * pair + 2, off:W],
                                   ACT.Exp, scale=SCALE).then_inc(z["exp_done"], 1)
                done = [t for t in range(NB) if q == min(T_END[t] + 1, NQ - 1)]
                for t in done:
                    act.wait_ge(z["pv_done"], PV_C + NQ * g + T_END[t] + 1)
                    act.wait_ge(z["ring_ready"], base + entry_after(plan, "turn", t - 2) if t >= 2 else base)
                    act.activation(OT[:, t % 2, :], ps[:, ACC, :], ACT.Copy).then_inc(z["ot_copied"], 1)

        def act_store(act, L, i):
            z = sems[L]
            act.wait_ge(z["row_act"], i + 1)
            act.wait_ge(z["row_dve"], i + 1)
            act.dma_start(rows_s[L][P * i:P * i + P, :], row[:, i % NROW, 0:QKV[L]]).then_inc(z["scr"][i % NROW], 16)

        def act_rows(act, L, T):
            z = sems[L]
            for i in range(TB * T, TB * T + TB):
                act.wait_ge(z["qkv_mm"], i + 1)
                if i >= NROW:
                    act.wait_ge(z["scr"][i % NROW], 16 * (i // NROW))
                split = (VOFF[0], W)[L]
                act.activation(row[:, i % NROW, split:QKV[L]], ps[:, 2 * (i % 2) + 1, 0:QKV[L] - split], ACT.Copy)\
                    .then_inc(z["row_act"], 1)
                act_store(act, L, i)

        @block.scalar
        def _(act):
            for L in range(2):
                z = sems[L]
                act.sem_inc(z["exp_done"], EXP_C)
                act.sem_inc(z["ot_copied"], OTC_C)
                for T in range(NB):
                    act_rows(act, L, T)
                with act.Fori(0, NG - 1) as g:
                    act_stage(act, L, g, STAGE, NLOW + NE * g)
                act_stage(act, L, NG - 1, LAST, BASE_LAST)
                for T in range(NB):
                    act.wait_ge(z["oT_ready"], 2 * T + 2)
                    act.activation(OcT[:, 1, W * T:W * T + W], ps[:, 5, :], ACT.Copy).then_inc(z["oT_copied"], 1)
                for T in range(NB):
                    act.wait_ge(z["stat_done"], T + 1)
                    act.activation(rstd[:, TB * T:TB * T + TB], rstd[:, TB * T:TB * T + TB], ACT.Sqrt)\
                        .then_inc(z["sq_done"], 1)
                for T in range(NB):
                    def x_copy(T):
                        act.wait_ge(z["xT_ready"], 2 * T + 2)
                        act.activation(xT[:, 1, W * T:W * T + W], ps[:, 5, :], ACT.Copy).then_inc(z["xT_copied"], 1)
                    if T == 0:
                        x_copy(0)
                    for n in range(FC[L]):
                        k = FC[L] * T + n
                        act.wait_ge(z["gu_ready"], k + 1)
                        if k >= 2:
                            act.wait_ge(z["hid_done"], k - 1)
                        act.activation(sl[:, n % 2, :], ps[:, 2 * (n % 2), :], ACT.Silu,
                                       scale=gs[:, n:n + 1] if L == 0 else 1.0).then_inc(z["silu_done"], 1)
                    if T + 1 < NB:
                        x_copy(T + 1)
                for T in range(NB):
                    act.wait_ge(z["stat2_done"], T + 1)
                    act.activation(rstd[:, TB * T:TB * T + TB], rstd[:, TB * T:TB * T + TB], ACT.Sqrt)\
                        .then_inc(z["sq2_done"], 1)
                if L == 0:
                    for T in range(NB):
                        act.wait_ge(z["x2T_ready"], 2 * T + 2)
                        act.activation(xT[:, 1, W * T:W * T + W], ps[:, 5, :], ACT.Copy)\
                            .then_inc(z["x2T_copied"], 1)

        def dve_row(dve, L, i):
            z = sems[L]
            dve.wait_ge(z["qkv_mm"], i + 1)
            r = i % NROW
            if i >= NROW:
                dve.wait_ge(z["scr"][r], 16 * (i // NROW))
            b = 2 * (i % 2)
            if L == 1:
                dve.tensor_copy(row[:, r, 0:W], ps[:, b, :]).then_inc(z["row_dve"], 1)
                return
            nh = ROPE // HD
            src = ps[:, b, 0:ROPE].rearrange("p (h d) -> p h d", d=HD)
            pairs = ps[:, b, 0:ROPE].rearrange("p (h d e) -> p h d e", d=HD // 2, e=2)
            rbp = rb.rearrange("p (h d e) -> p h d e", d=HD // 2, e=2)
            cos = rope[:, i, None, 0:HD].to_broadcast([P, nh, HD])
            sn = rope[:, i, HD:2 * HD].rearrange("p (d e) -> p d e", e=2)
            if i >= 1:
                dve.wait_ge(z["row_dve"], i)
            dve.tensor_tensor(ra.rearrange("p (h d) -> p h d", d=HD), src, cos, ALU.mult).then_inc(z["rope_a"], 1)
            for e in range(2):
                dve.tensor_tensor(rbp[:, :, :, e], pairs[:, :, :, 1 - e],
                                  sn[:, None, :, e].to_broadcast([P, nh, HD // 2]), ALU.mult).then_inc(z["rope_b"], 1)
            dve.wait_ge(z["rope_a"], i + 1)
            dve.wait_ge(z["rope_b"], 2 * (i + 1))
            dve.tensor_tensor(row[:, r, 0:ROPE], ra, rb, ALU.add).then_inc(z["row_dve"], 1)

        def dve_unit(dve, L, unit, e, bank):
            z = sems[L]
            c, i, heads = unit
            w = width(c, i)
            dve.wait_ge(z["ring_ready"], e + 1)
            dve.tensor_reduce(pm[:, i // TB, i % TB, heads[0]:heads[-1] + 1, c],
                              ps[:, bank, 0:w * len(heads)].rearrange("p (h w) -> p h w", w=w), AX.X, ALU.max)\
                .then_inc(z["ring_read"], 1)

        def dve_neg_max(dve, L, n, T, entries):
            z = sems[L]
            dve.wait_ge(z["ring_read"], entries)
            if not (isinstance(n, int) and n == 0):
                dve.wait_ge(z["shift_done"], block_index(n - 1, T) + 1)
            dve.tensor_reduce(negm[:, T, :, :], pm[:, T, :, :, 0:T + 1], AX.X, ALU.max, negate=True)\
                .then_inc(z["neg_max"], 1)

        def dve_norm(dve, L, g, T, e, bank):
            z = sems[L]
            tr = ps[:, bank, :].rearrange("p (t h c) -> p t h c", t=TB, h=HG)
            dve.wait_ge(z["ring_ready"], e + 1)
            dve.reciprocal(rden[:, T, :, :], tr[:, :, :, HD]).then_inc(z["o_step"], 1)
            dve.wait_ge(z["o_step"], NB * g + T + 1)
            dve.tensor_tensor(O[:, TB * T:TB * T + TB, bass.ds(g * (HG * HD), HG * HD)]
                              .rearrange("p t (h d) -> p t h d", d=HD), tr[:, :, :, 0:HD],
                              rden[:, T, :, :, None].to_broadcast([P, TB, HG, HD]), ALU.mult).then_inc(z["ring_read"], 1)

        def dve_stage(dve, L, g, plan, base, meanwhile=None):
            for e, (what, k) in enumerate(entries_of(plan)):
                bank = RING[(NLOW + e) % len(RING)]
                if what == "turn":
                    if meanwhile:
                        meanwhile(k)
                    dve_norm(dve, L, g, k, base + e, bank)
                    continue
                dve_unit(dve, L, UNITS[k], base + e, bank)
                T = UNITS[k][1] // TB
                if k + 1 == len(UNITS) or UNITS[k + 1][1] // TB != T:
                    dve_neg_max(dve, L, g if T == TOP else g + 1, T, base + e + 1)

        def quantise(dve, w, n, st):
            a, b = tmpa[:, 0:n], tmpb[:, 0:n]

            def step(ins):
                st[0] += 1
                ins.then_inc(quant_step, 1)
                dve.wait_ge(quant_step, st[0])

            step(dve.tensor_scalar(a.bitcast(INT32), w.bitcast(INT32), 0x7F800000, None, ALU.bitwise_and))
            step(dve.tensor_scalar(a, a, 2.0 ** -6, 1.5 * 2.0 ** 20, ALU.max, ALU.mult))
            step(dve.tensor_tensor(b, w, a, ALU.add))
            step(dve.tensor_tensor(w, b, a, ALU.subtract))
            step(dve.tensor_tensor(b, w, w, ALU.mult))
            step(dve.tensor_scalar(a, b, 448.0 ** 2, 3.0e38, ALU.is_gt, ALU.mult))
            step(dve.tensor_tensor(b, a, a, ALU.mult))
            step(dve.tensor_tensor(b, b, b, ALU.subtract))
            step(dve.tensor_tensor(w, w, b, ALU.add))

        @block.vector
        def _(dve):
            for L in range(2):
                z = sems[L]
                if L == 0:
                    dve.wait_ge(c_in, 16)
                for what, k in FIRST:
                    if what == "rows":
                        for i in range(TB * k, TB * k + TB):
                            dve_row(dve, L, i)
                        continue
                    dve_unit(dve, L, LOW[k], k, RING[k % len(RING)])
                    T = LOW[k][1] // TB
                    if k + 1 == NLOW or LOW[k + 1][1] // TB != T:
                        dve_neg_max(dve, L, 0, T, k + 1)
                with dve.Fori(0, NG - 1) as g:
                    dve_stage(dve, L, g, STAGE, NLOW + NE * g)
                if L == 0:
                    chunks = [WG[0][:, c, :] for c in range(DC)] + [WU[0][:, c, :] for c in range(DC)]
                    dn = WD[0].rearrange("p c n -> p (c n)")
                    chunks += [dn[:, 0:768], dn[:, 768:1536]]
                    st = [0]

                    def round_weights(T):
                        if T < TOP - 1:
                            return
                        if T == TOP - 1:
                            dve.wait_ge(sems[0]["ffw"], 48)
                        for w in chunks[0:3] if T == TOP - 1 else chunks[3:6]:
                            quantise(dve, w, 768, st)

                    dve_stage(dve, L, NG - 1, LAST, BASE_LAST, round_weights)
                else:
                    dve_stage(dve, L, NG - 1, LAST, BASE_LAST)
                if L == 0:
                    dve.sem_inc(quant_done, 3)
                if L == 0:
                    dve.wait_ge(x_in, 16)
                for T in range(NB):
                    dve.wait_ge(z["oT_ready"], 2 * T + 1)
                    dve.tensor_copy(OcT[:, 0, W * T:W * T + W], ps[:, 4, :]).then_inc(z["oT_copied"], 1)
                    for t in range(TB):
                        i = TB * T + t
                        dve.wait_ge(z["y_ready"], 2 * T + t // 2 + 1)
                        y = ps[:, 2 * (T % 2) + t // 2, D * (t % 2):D * (t % 2) + D]
                        dve.tensor_tensor(X[:, i, :], y, X[:, i, :], ALU.add).then_inc(z["res_done"], 1)
                        dve.wait_ge(z["res_done"], i + 1)
                        dve.bn_stats(stats[:, i, :], X[:, i, :]).then_inc(z["stat_step"], 1)
                        dve.wait_ge(z["stat_step"], 2 * i + 1)
                        dve.bn_aggr(mv[:, i, :], stats[:, i, :]).then_inc(z["stat_step"], 1)
                    dve.wait_ge(z["stat_step"], 2 * TB * (T + 1))
                    dve.tensor_scalar(rstd[:, TB * T:TB * T + TB], mv[:, TB * T:TB * T + TB, 1], EPS, None, ALU.add)\
                        .then_inc(z["stat_done"], 1)
                for T in range(NB):
                    dve.wait_ge(z["sq_done"], T + 1)
                    dve.reciprocal(rstd[:, TB * T:TB * T + TB], rstd[:, TB * T:TB * T + TB]).then_inc(z["rs_step"], 1)
                    dve.wait_ge(z["rs_step"], T + 1)
                    for t in range(TB):
                        i = TB * T + t
                        dve.tensor_scalar(X[:, i, :], X[:, i, :], mv[:, i, 0:1], rstd[:, i:i + 1], ALU.subtract,
                                          ALU.mult).then_inc(z["ln_done"], 1)

                def x_copy(T):
                    dve.wait_ge(z["xT_ready"], 2 * T + 1)
                    dve.tensor_copy(xT[:, 0, W * T:W * T + W], ps[:, 4, :]).then_inc(z["xT_copied"], 1)

                x_copy(0)
                for T in range(NB):
                    for n in range(FC[L]):
                        k = FC[L] * T + n
                        if n == 0 and T >= 2:
                            dve.wait_ge(z["down_ready"], 2 * (T - 1))
                        dve.wait_ge(z["silu_done"], k + 1)
                        dve.wait_ge(z["gu_ready"], k + 1)
                        up = ps[:, 2 * (n % 2) + 1, :]
                        if L == 0:
                            dve.scalar_tensor_tensor(out=hid[T % 2][:, n, :], in0=up, scalar=us[:, n:n + 1],
                                                     in1=sl[:, n % 2, :], op0=ALU.mult, op1=ALU.mult)\
                                .then_inc(z["hid_done"], 1)
                        else:
                            dve.tensor_tensor(hid[T % 2][:, n, :], up, sl[:, n % 2, :], ALU.mult)\
                                .then_inc(z["hid_done"], 1)
                    if T + 1 < NB:
                        x_copy(T + 1)
                    for t in range(TB):
                        i = TB * T + t
                        if t % 2 == 0:
                            dve.wait_ge(z["down_ready"], 2 * T + t // 2 + 1)
                        y = ps[:, 6 + t // 2, D * (t % 2):D * (t % 2) + D]
                        if L == 0:
                            dve.tensor_tensor(yt[:, t % 2, :], y, ds[:, :], ALU.mult).then_inc(z["y_scaled"], 1)
                            dve.wait_ge(z["y_scaled"], i + 1)
                            y = yt[:, t % 2, :]
                        dve.tensor_tensor(X[:, i, :], y, X[:, i, :], ALU.add).then_inc(z["res2_done"], 1)
                        dve.wait_ge(z["res2_done"], i + 1)
                        dve.bn_stats(stats[:, i, :], X[:, i, :]).then_inc(z["stat2_step"], 1)
                        dve.wait_ge(z["stat2_step"], 2 * i + 1)
                        dve.bn_aggr(mv[:, i, :], stats[:, i, :]).then_inc(z["stat2_step"], 1)
                    dve.wait_ge(z["stat2_step"], 2 * TB * (T + 1))
                    dve.tensor_scalar(rstd[:, TB * T:TB * T + TB], mv[:, TB * T:TB * T + TB, 1], EPS, None, ALU.add)\
                        .then_inc(z["stat2_done"], 1)
                for T in range(NB):
                    dve.wait_ge(z["sq2_done"], T + 1)
                    dve.reciprocal(rstd[:, TB * T:TB * T + TB], rstd[:, TB * T:TB * T + TB]).then_inc(z["rs2_step"], 1)
                    dve.wait_ge(z["rs2_step"], T + 1)
                    for t in range(TB):
                        i = TB * T + t
                        dve.tensor_scalar(X[:, i, :], X[:, i, :], mv[:, i, 0:1], rstd[:, i:i + 1], ALU.subtract,
                                          ALU.mult).then_inc(z["ln2_done"], 1)
                if L == 0:
                    for T in range(NB):
                        dve.wait_ge(z["x2T_ready"], 2 * T + 1)
                        dve.tensor_copy(xT[:, 0, W * T:W * T + W], ps[:, 4, :]).then_inc(z["x2T_copied"], 1)


def _rope_table():
    inv_freq = np.float32(1.0) / np.power(np.float32(10000.0), np.arange(0, HD, 2, dtype=np.float32) / np.float32(HD))
    angle = np.arange(S, dtype=np.float32)[:, None] * inv_freq[None, :].astype(np.float32)
    cos, sin = np.cos(angle), np.sin(angle)
    return np.concatenate([np.repeat(cos, 2, axis=1), np.stack([-sin, sin], axis=-1).reshape(S, HD)],
                          axis=1).astype(np.float32)


def kernel(**inputs):
    import concourse.bacc as _bacc
    from concourse import mybir as _mybir
    from concourse.bass_utils import run_bass_kernel_spmd as _run

    i = inputs
    host = {
        "x": i["L0_attn_x"][0],
        "xT": i["L0_attn_x"][0].T,
        "wqkv0": np.concatenate([i["L0_attn_Wq"].T, i["L0_attn_Wk"].T, i["L0_attn_Wv"].T], axis=1),
        "wqkv1": np.concatenate([i["L1_attn_wq"].T, i["L1_attn_wk"].T, i["L1_attn_wv"].T], axis=1),
        "bqkv": np.concatenate([i["L0_attn_bq"], i["L0_attn_bk"], i["L0_attn_bv"]])[None, :],
        "wo0": i["L0_attn_Wo"].T,
        "wo1": i["L1_attn_wo"].T,
        "bo": i["L0_attn_bo"][None, :],
        "gate0": i["L0_ffn_gate_w"],
        "gate1": i["L1_ffn_w_gate"].T,
        "up0": i["L0_ffn_up_w"],
        "up1": i["L1_ffn_w_up"].T,
        "down0": i["L0_ffn_down_w"],
        "down1": i["L1_ffn_w_down"].T,
        "gs": i["L0_ffn_gate_scale"].reshape(FC[0], P).T,
        "us": i["L0_ffn_up_scale"].reshape(FC[0], P).T,
        "ds": i["L0_ffn_down_scale"][None, :],
        "rope": _rope_table(),
    }
    nc = _bacc.Bacc("TRN2", target_bir_lowering=False, num_devices=1)
    arrays, t = {}, {}
    for name, a in host.items():
        a = np.ascontiguousarray(a)
        arrays[f"in_{name}_dram"] = a
        t[name] = nc.dram_tensor(f"in_{name}_dram", a.shape, _mybir.dt.from_np(a.dtype), kind="ExternalInput").ap()
    out = nc.dram_tensor("out_0_dram", (1, S, D), FP32, kind="ExternalOutput").ap()
    network_kernel(nc, t["x"], t["xT"], (t["wqkv0"], t["wqkv1"]), t["bqkv"], (t["wo0"], t["wo1"]), t["bo"],
                   (t["gate0"], t["gate1"]), (t["up0"], t["up1"]), (t["down0"], t["down1"]), t["gs"], t["us"],
                   t["ds"], t["rope"], out[0])
    r = _run(nc, [arrays], core_ids=[0])
    return r.results[0]["out_0_dram"]
```

```python
import numpy as np
import concourse.bass as bass
from concourse import mybir
from contextlib import ExitStack


FP32 = mybir.dt.float32
BF16 = mybir.dt.bfloat16
INT32 = mybir.dt.int32
ACT = mybir.ActivationFunctionType
ALU = mybir.AluOpType
AX = mybir.AxisListType

P = 128
S = 2048
D = 256
DC = D // P
NT = S // P
TB = 4
NB = NT // TB
W = TB * P
HD = 16
HEADS = 16
HG = 4
NG = HEADS // HG
SCALE = HD ** -0.5
EPS = 1e-5
KVW = (HD, HG * HD)
KH = (1, HG)
KV = (NG * HD, HEADS * HD)
VOFF = (HEADS * HD + KV[0], HEADS * HD + KV[1])
SWAPPED = VOFF[0] + KV[0]
WIDTHS = (SWAPPED + HEADS * HD + KV[0], 3 * HEADS * HD)
PROJ = (((0, SWAPPED, P), (P, SWAPPED + P, P), (2 * P, SWAPPED + 2 * P, KV[0])),
        tuple((P * c, None, P) for c in range(4)))
NPROJ = (len(PROJ[0]), len(PROJ[1]))
PARTS = 3
PR = PARTS * HD
SLOTS = 3
FF = (768, 1024)
FC = (FF[0] // P, FF[1] // P)
CHUNKS = 2 * (NG - 1)
CW = 3 * DC * FF[0] // CHUNKS
ROUND = 8
AK = 16 * 6
AQ = 16 * 3
BK = 16 * (1 + TB)
BQ = 16 * 2
NEG = -1e30

QUADS = [(T, j, max(0, P * (j - TB * T))) for T in range(NB) for j in range(TB * T + TB)]
NQ = len(QUADS)
T_END = [max(q for q in range(NQ) if QUADS[q][0] == T) for T in range(NB)]
KEYS_END = [max(q for q in range(NQ) if QUADS[q][1] // TB == c) for c in range(NB)]


def width(c, i):
    return min(W, P * (i + 1) - W * c)


def units_of(T):
    out = []
    for c in range(T + 1):
        for i in range(TB * T, TB * T + TB):
            n = W // width(c, i) if width(c, i) in (P, W // 2) else 1
            if i == 1:
                n = 1
            out += [(c, i, tuple(range(h, h + n))) for h in range(0, HG, n)]
    return out


TOP = NB - 1
LOW = [u for T in range(TOP) for u in units_of(T)]
HIGH = units_of(TOP)
UNITS = HIGH + LOW
NHIGH = len(HIGH)
RING = (4, 5, 7)
TURN_AT = {T_END[T] + 2: T for T in range(TOP)}


def cols(u):
    return width(u[0], u[1]) * len(u[2])


_ends = [NHIGH - 1 + sum(len(units_of(t)) for t in range(T + 1)) for T in range(2)]
SHIFT_AFTER = {_ends[0] + 5: 0, _ends[1] + 7: 1}

DENSE_AT = {}
for _T in range(TOP):
    DENSE_AT[T_END[_T] + 3] = [("oT", _T, 0), ("oT", _T, 1)]
    DENSE_AT[T_END[_T] + 5] = [("y", _T, 0), ("y", _T, 1)]
DENSE_AT[18] = [("sqrt", 0), ("sqrt", 1)]
DENSE_AT[19] = [("ln", 0), ("ln", 1)]
DENSE_AT[20] = [("xT", 0, 0), ("xT", 0, 1), ("xT", 1, 0), ("xT", 1, 1)]
RINGED = ("low", "unit", "shift", "turn", "oT", "y", "xT", "down", "x2T")
SHIFT_TOP, SHIFT_TOP_LAST = 20, 18
POWERS = (("unit", 2), ("shift", 1))


def plan_stage(last):
    out, u, due, done = [], 0, 0, 0
    n_units, kept, pace = (NHIGH, 0, 3) if last else (len(UNITS), 4, 2)

    def fill():
        nonlocal u, done
        while u < n_units - kept and done + cols(UNITS[u]) // 2 <= due * pace // 2:
            done += cols(UNITS[u])
            out.append(("unit", u))
            if u in SHIFT_AFTER:
                out.append(("shift", SHIFT_AFTER[u]))
            u += 1

    for q in range(NQ):
        if q == 2:
            out.append(("shift", 2))
        if q == (SHIFT_TOP_LAST if last else SHIFT_TOP):
            assert u >= NHIGH
            out.append(("shift", TOP))
        for pair in range(2):
            out.append(("scores", q, pair))
            due += W - QUADS[q][2]
            fill()
        if q > 0:
            out.append(("pv", q - 1))
            due += 2 * (W - QUADS[q - 1][2])
            fill()
        if q in TURN_AT:
            out.append(("turn", TURN_AT[q]))
        if last:
            out += DENSE_AT.get(q, [])
    out.append(("pv", NQ - 1))
    if not last:
        out += [("unit", k) for k in range(u, n_units)]
        out.append(("turn", TOP))
    return out


def plan_after(L):
    out = [("sqrt", 2)]
    for T in range(NB):
        if T == 0:
            among = {0: [("turn", TOP)], 1: [("oT", TOP, 0), ("oT", TOP, 1), ("ln", 2)],
                     2: [("y", TOP, 0), ("y", TOP, 1)], 3: [("sqrt", TOP)], 4: [("ln", TOP)]}
            if L == 1:
                among[2] = [("xT", 2, 0), ("xT", 2, 1)] + among[2]
                among[5] = [("xT", TOP, 0), ("xT", TOP, 1)]
        else:
            at = 4 if L == 0 else 1
            among = {at: [("down", T - 1, 0), ("down", T - 1, 1)], at + 1: [("sqrt2", T - 1)]}
            if L == 1:
                among[3] = [("ln2", T - 1)]
            else:
                among[0] = []
                if T >= 2:
                    among[0] += [("ln2", T - 2)]
                    among[2] = [("x2T", T - 2, 0), ("x2T", T - 2, 1)]
                if T < TOP:
                    among[0] += [("xT", T + 1, 0), ("xT", T + 1, 1)]
        for n in range(FC[L]):
            out.append(("gu", T, n))
            out += among.get(n, [])
    return out


def ringed(plan):
    return [x for x in plan if x[0] in RINGED]


STAGE = plan_stage(False)
LAST = plan_stage(True)
NE = len(ringed(STAGE))
NFIRST = len(LOW) + 2
BASE_LAST = NFIRST + NE * (NG - 1)
assert NE % len(RING) == 0

_first_shifts = {_ends[0] - NHIGH + 14: 0, _ends[1] - NHIGH + 18: 1}
_low = []
for _k in range(len(LOW)):
    _low.append(("low", _k))
    if _k + NHIGH in _ends:
        _low.append(("split", _ends.index(_k + NHIGH)))
    if _k in _first_shifts:
        _low.append(("shift", _first_shifts[_k]))
_cuts = [_low.index(("low", sum(len(units_of(t)) for t in range(T)))) for T in range(TOP)] + [len(_low)]
_lows = [_low[_cuts[T]:_cuts[T + 1]] for T in range(TOP)]
_end = [("down", TOP, 0), ("down", TOP, 1)]
_norm = [("sqrt2", TOP), ("ln2", TOP)]
_x2T = [("x2T", T, c) for T in (2, TOP) for c in range(DC)]


def spread(steps, among):
    out = []
    for k, step in enumerate(steps):
        out.append(step)
        out += among[len(among) * k // len(steps):len(among) * (k + 1) // len(steps)]
    return out


def plan_first(L):
    block = []
    for T in range(NB):
        steps = [("proj", T, j, half) for j in range(NPROJ[L]) for half in range(2)]
        steps[2:2] = [("values", T, 0)]
        steps[5:5] = [("values", T, 1)]
        block.append(steps + [("flush", T)])
    if L == 0:
        return block[0] + block[1] + spread(block[2], _lows[0]) + spread(block[3], _lows[1]) + _lows[2]
    return (block[0][:2] + [("ln2", 2)] + block[0][2:6] + _x2T[0:2] + block[0][6:] + _end + block[1][:6] + _norm[:1] +
            block[1][6:] + _norm[1:] + block[2][:3] +
            _x2T[2:4] + spread(block[2][3:], _lows[0]) + spread(block[3], _lows[1]) + _lows[2])


FIRST = (plan_first(0), plan_first(1))
AFTER = (plan_after(0), plan_after(1) + _end + _norm)
_carried = [x for x in FIRST[1] if x[0] in ("down", "x2T")]
TAIL = tuple(ringed(LAST + AFTER[L] + (_carried if L == 0 else [])) for L in range(2))


def first_entry(*item):
    return 1 + ringed(_low).index(item)


def entry_after(plan, *item):
    return 1 + ringed(plan).index(item)


def tail_entry(L, *item):
    return BASE_LAST + 1 + TAIL[L].index(item)


def high_end(c):
    return entry_after(STAGE, "unit", max(k for k in range(NHIGH) if UNITS[k][0] == c))


def block_index(n, T):
    return NB * n + T


def network_kernel(nc, x, xT_d, wqkv_d, bqk_d, bv_d, wo_d, bo_d, gate_d, up_d, down_d,
                   gs_d, us_d, ds_d, rope_d, out):
    ctx = ExitStack()
    with ctx:
        def sb(name, shape, dt=FP32):
            return ctx.enter_context(nc.sbuf_tensor(name, shape, dt))

        def sem(name):
            return ctx.enter_context(nc.semaphore(name))

        X = sb("X", [P, NT, D])
        O = sb("O", [P, NT, D])
        xT = sb("xT", [P, DC, S])
        maxbuf = sb("maxbuf", [P, 2 * 4096])
        KT1 = maxbuf[:, 0:4096].bitcast(BF16).rearrange("p (T h w) -> p T h w", T=NB, h=HG)
        QT1 = maxbuf[:, 4096:8192].bitcast(BF16).rearrange("p (T h w) -> p T h w", T=NB, h=HG)
        spvbuf = sb("spvbuf", [P, 2 * 4096])
        KT2 = spvbuf[:, 0:4096].bitcast(BF16).rearrange("p (T h w) -> p T h w", T=NB, h=HG)
        QT2 = spvbuf[:, 4096:8192].bitcast(BF16).rearrange("p (T h w) -> p T h w", T=NB, h=HG)
        PB = sb("PB", [P, 2, HG, W])
        VG = sb("VG", [P, NT, HG, 32])
        OT = sb("OT", [P, 2, W])
        wqkv = sb("wqkv", [P, DC, WIDTHS[1]])
        wo = sb("wo", [P, DC, D])
        bqk = sb("bqk", [P, 2 * NPROJ[0]])
        bv = sb("bv", [1, KV[0]])
        bo = sb("bo", [1, D])
        ones_row = sb("ones_row", [1, P])
        early = sb("early", [P, 6144])
        rope = early[:, 0:4096].rearrange("p (a s) -> p a s", a=2)
        ra = early[:, 4096:4096 + W]
        rb = early[:, 4096 + W:4096 + 2 * W]
        rf = early[:, 5120:6144].rearrange("p (r w) -> p r w", r=2)
        raw = early[:, 0:(CHUNKS + 1) * CW].rearrange("p (k n) -> p k n", n=CW)
        rounded = early[:, 0:(CHUNKS + 1) * CW].bitcast(BF16).rearrange("p (k n) -> p k n", n=2 * CW)
        rest = sb("rest", [P, 2, W])
        work = sb("work", [P, SLOTS * PARTS * W // 2])
        parts = work[:, :].bitcast(BF16).rearrange("p (r k w) -> p r k w", r=SLOTS, k=PARTS)
        tmpa, tmpb = work[:, 0:CW], work[:, CW:2 * CW]
        hf = work[:, 0:2 * W].rearrange("p (r w) -> p r w", r=2)
        hrest = work[:, 2 * W:4 * W].rearrange("p (r w) -> p r w", r=2)
        vrow = sb("vrow", [P, TB, KV[1]])
        sh = sb("sh", [P, 2, PARTS * HG * TB], BF16)
        shT = sb("shT", [PARTS * HG * TB, 2, P], BF16)
        pm = sb("pm", [P, NB, TB, HG, NB])
        negm = sb("negm", [P, NB, TB, HG])
        rm = sb("rm", [P, TB, HG])
        rden = sb("rden", [P, NB, TB, HG])
        stats = sb("stats", [P, NT, 6])
        mv = sb("mv", [P, NT, 2])
        rstd = sb("rstd", [P, 2, NT])
        ident = sb("ident", [P, P])
        identb = sb("identb", [P, P], BF16)
        mask_qk = sb("mask_qk", [P, P], BF16)
        mask_kq = sb("mask_kq", [P, P], BF16)
        gs = sb("gs", [P, FC[0]])
        us = sb("us", [P, FC[0]])
        ds = sb("ds", [P, D])
        sl = sb("sl", [P, 2, W])
        yt = sb("yt", [P, 2, D])
        pb_flat = PB[:, :, :, :].rearrange("p a h w -> p (a h w)")
        WG = maxbuf[:, 0:2048].rearrange("p (c n) -> p c n", c=DC)
        WU = maxbuf[:, 2048:4096].rearrange("p (c n) -> p c n", c=DC)
        WD = maxbuf[:, 4096:4096 + FC[1] * D].rearrange("p (c n) -> p c n", c=FC[1])
        xp = maxbuf[:, 0:3072].bitcast(BF16).rearrange("p (r c k w) -> p r c k w", r=2, c=DC, k=PARTS)
        hp_even = maxbuf[:, 3072:7680].bitcast(BF16).rearrange("p (k n w) -> p k n w", k=PARTS, n=FC[0])
        hp_odd = pb_flat[:, 0:3072].bitcast(BF16).rearrange("p (k n w) -> p k n w", k=2, n=FC[0])
        hp_odd_low = spvbuf[:, 4096:4096 + 1536].bitcast(BF16).rearrange("p (n w) -> p n w", n=FC[0])

        def hp(T, k, n):
            if T % 2 == 0:
                return hp_even[:, k, n, :]
            return hp_odd[:, k, n, :] if k < 2 else hp_odd_low[:, n, :]
        hid = [PB[:, :, :, :].rearrange("p a h w -> p (a h) w"),
               spvbuf[:, 4096:8192].rearrange("p (n w) -> p n w", w=W)]

        ps = ctx.enter_context(nc.psum_tensor("ps", [P, 8, W], FP32))
        ACC = 6

        q_s = [nc.dram_tensor(f"q_s{L}", [NG, HG, PR, S], BF16).ap() for L in range(2)]
        k_s = [nc.dram_tensor(f"k_s{L}", [NG, KH[L], PR, S], BF16).ap() for L in range(2)]
        v_s = [nc.dram_tensor(f"v_s{L}", [S, KV[L]], FP32).ap() for L in range(2)]

        names = ("proj_ready proj_read hi_done mid_done lo_done v_ready v_copied v_stored "
                 "ring_ready ring_read neg_max shift_step shift_done "
                 "s_ready exp_done pv_done ot_copied o_step "
                 "ln_step var_done sqrt_done ln_done var2_done sqrt2_done gu_ready silu_done hid_done ln2_done").split()
        only0 = "rope_a rope_f rest_done xmid_done xlow_done h_done hhigh_done hrest_done hmid_done power_done round_step".split()

        sems = []
        for L in range(2):
            s = {n: sem(f"{n}{L}") for n in names + (only0 if L == 0 else [])}
            for kind in ("ak", "aq", "bk", "bq"):
                for T in range(NB):
                    s[kind, T] = sem(f"{kind}{T}_{L}")
            s["stored"] = [sem(f"stored{r}_{L}") for r in range(SLOTS)]
            s["ffw"] = sem(f"ffw{L}")
            s["wload"] = sem(f"wload{L}")
            sems.append(s)
        x_in = sem("x_in")
        xT_in = [sem(f"xT_in{T}") for T in range(NB)]
        w_in = sem("w_in")
        b_in = sem("b_in")
        rope_in = [sem(f"rope_in{T}") for T in range(NB)]
        const_step = sem("const_step")
        passed_sp = sem("passed_sp")
        passed_pool = sem("passed_pool")
        fill_step = sem("fill_step")
        out_done = sem("out_done")

        EXP_C, PV_C, OTC_C, ROUND_C = 2, 2, 1, 1

        def wait_count(eng, passed, sem_, value):
            eng.wait_ge(sem_, value)
            eng.sem_inc(passed, 1)

        block = ctx.enter_context(nc.Block())

        def units_before(L, T, r):
            return len([u for u in range(NPROJ[L] * T) if u % SLOTS == r])

        def sp_stored(sp, L, T):
            z = sems[L]
            for r in range(SLOTS):
                sp.wait_ge(z["stored"][r], 16 * PARTS * units_before(L, T + 1, r))
            sp.wait_ge(z["v_stored"], 16 * (T + 1))

        def sp_max_keys(sp, L, n, T, entries=None):
            z = sems[L]
            if entries is not None:
                wait_count(sp, passed_sp, z["ring_ready"], entries)
                wait_count(sp, passed_sp, z["bk", T], BK * n)
            for slot, k in enumerate((0, 0, 0, 1, 1, 2)):
                sp.dma_start(KT1[HD * slot:HD * slot + HD, T, 0:KH[L], :],
                             k_s[L][n, :, HD * k:HD * k + HD, W * T:W * T + W].rearrange("h r w -> r h w"))\
                    .then_inc(z["ak", T], 16)

        def sp_max_queries(sp, L, n, T, entries=None):
            z = sems[L]
            if entries is not None:
                wait_count(sp, passed_sp, z["ring_ready"], entries)
                wait_count(sp, passed_sp, z["bq", T], BQ * n)
            for first, rows in ((0, 3 * HD), (3 * HD, 2 * HD), (5 * HD, HD)):
                sp.dma_start(QT1[first:first + rows, T, :, :],
                             q_s[L][n, :, 0:rows, W * T:W * T + W].rearrange("h r w -> r h w"))\
                    .then_inc(z["aq", T], 16)

        def sp_spv_keys(sp, L, n, T, quads=None):
            z = sems[L]
            if quads is not None:
                wait_count(sp, passed_sp, z["pv_done"], PV_C + quads)
            wait_count(sp, passed_sp, z["ak", T], AK * (n + 1))
            sp.dma_start(KT2[0:6 * HD, T, 0:KH[L], :], KT1[0:6 * HD, T, 0:KH[L], :]).then_inc(z["bk", T], 16)
            for i in range(TB * T, TB * T + TB):
                sp.dma_start(VG[:, i, 0:KH[L], 0:HD],
                             v_s[L][P * i:P * i + P, bass.ds(n * KVW[L], KVW[L])].rearrange("p (h d) -> p h d", d=HD))\
                    .then_inc(z["bk", T], 16)

        def sp_spv_queries(sp, L, n, T, quads=None):
            z = sems[L]
            if quads is not None:
                wait_count(sp, passed_sp, z["pv_done"], PV_C + quads)
            wait_count(sp, passed_sp, z["aq", T], AQ * (n + 1))
            sp.dma_start(QT2[0:6 * HD, T, :, :], QT1[0:6 * HD, T, :, :]).then_inc(z["bq", T], 16)

        def sp_shift(sp, L, T, entries):
            z = sems[L]
            wait_count(sp, passed_sp, z["ring_read"], entries)
            sp.dma_start(QT2[6 * HD:6 * HD + PARTS, T, :, :].rearrange("p h (t w) -> p (h t) w", w=P),
                         shT[:, T % 2, :]).then_inc(z["bq", T], 16)

        def sp_stage(sp, L, g):
            m = g + 1
            base = NFIRST + NE * g

            def keys(T):
                sp_max_keys(sp, L, m, T, base + high_end(T))

            sp_spv_queries(sp, L, g, TOP, NQ * g)
            sp_max_queries(sp, L, m, 0, base)
            sp_max_queries(sp, L, m, 1, base)
            sp_shift(sp, L, 2, base + entry_after(STAGE, "shift", 2))
            keys(0)
            sp_max_queries(sp, L, m, 2, base)
            keys(1)
            keys(2)
            sp_spv_queries(sp, L, m, 0, NQ * g + T_END[0] + 1)
            sp_spv_queries(sp, L, m, 1, NQ * g + T_END[1] + 1)
            sp_shift(sp, L, TOP, base + entry_after(STAGE, "shift", TOP))
            keys(TOP)
            sp_max_queries(sp, L, m, TOP, base + high_end(TOP))
            sp_shift(sp, L, 0, base + entry_after(STAGE, "shift", 0))
            sp_spv_queries(sp, L, m, 2, NQ * g + T_END[2] + 1)
            sp_shift(sp, L, 1, base + entry_after(STAGE, "shift", 1))
            for T in range(NB):
                sp_spv_keys(sp, L, m, T, NQ * g + KEYS_END[T] + 1)

        @block.sync
        def _(sp):
            for c in range(DC):
                sp.dma_start(wqkv[:, c, 0:WIDTHS[0]], wqkv_d[0][c * P:c * P + P, :]).then_inc(w_in, 16)
            sp.dma_start(bqk[:, :], bqk_d[:, :]).then_inc(w_in, 16)
            sp.dma_start(bv[:, :], bv_d[:, :]).then_inc(w_in, 16)
            for T in range(NB):
                for c in range(DC):
                    sp.dma_start(xT[:, c, W * T:W * T + W], xT_d[c * P:c * P + P, W * T:W * T + W])\
                        .then_inc(xT_in[T], 16)
                sp.dma_start(rope[:, :, W * T:W * T + W], rope_d[:, :, W * T:W * T + W]).then_inc(rope_in[T], 16)
            for L in range(2):
                z = sems[L]
                for T in range(NB):
                    sp_stored(sp, L, T)
                    sp_max_queries(sp, L, 0, T)
                    sp_max_keys(sp, L, 0, T)
                if L == 0:
                    for k, w in enumerate((gate_d[0], up_d[0], down_d[0])):
                        sp.dma_start(raw[:, 2 * k + 1:2 * k + 3, :].rearrange("p k n -> p (k n)"),
                                     w.rearrange("(c p) n -> p c n", p=P)).then_inc(z["ffw"], 16)
                if L == 1:
                    sp.wait_ge(sems[0]["ring_ready"], tail_entry(0, "down", TOP, 1))
                for T in range(TOP):
                    sp_spv_keys(sp, L, 0, T)
                    sp_spv_queries(sp, L, 0, T)
                sp_spv_keys(sp, L, 0, TOP)
                for T in range(2):
                    sp_shift(sp, L, T, first_entry("shift", T))
                with sp.Fori(0, NG - 1) as g:
                    sp_stage(sp, L, g)
                sp_spv_queries(sp, L, NG - 1, TOP, NQ * (NG - 1))
                sp.dma_start(wo[:, :, :], wo_d[L].rearrange("(c p) n -> p c n", p=P)).then_inc(z["wload"], 16)
                if L == 0:
                    sp.dma_start(X[:, :, :], x.rearrange("(t p) c -> p t c", p=P)).then_inc(x_in, 16)
                    sp.dma_start(bo[:, :], bo_d[:, :]).then_inc(b_in, 16)
                    sp.dma_start(gs[:, :], gs_d[:, :]).then_inc(b_in, 16)
                    sp.dma_start(us[:, :], us_d[:, :]).then_inc(b_in, 16)
                    sp.dma_start(ds[:, :], ds_d[0:1, :].to_broadcast([P, D]))\
                        .then_inc(b_in, 16)
                    for c in range(DC):
                        sp.dma_start(wqkv[:, c, :], wqkv_d[1][c * P:c * P + P, :]).then_inc(sems[1]["wload"], 16)
                for T in (2, TOP):
                    sp_shift(sp, L, T, BASE_LAST + entry_after(LAST, "shift", T))
                if L == 0:
                    sp.wait_ge(z["ring_ready"], tail_entry(0, "y", TOP, 1))
                    continue
                sp.wait_ge(z["ring_ready"], tail_entry(L, "unit", NHIGH - 1))
                sp.wait_ge(z["bq", TOP], BQ * NG)
                sp.dma_start(WG, gate_d[L].rearrange("(c p) n -> p c n", p=P)).then_inc(z["ffw"], 16)
                sp.dma_start(WU, up_d[L].rearrange("(c p) n -> p c n", p=P)).then_inc(z["ffw"], 16)
                sp.dma_start(WD, down_d[L].rearrange("(c p) n -> p c n", p=P)).then_inc(z["ffw"], 16)
            for i in range(0, NT, 2):
                sp.wait_ge(sems[1]["ln2_done"], i + 2)
                sp.dma_start(out[P * i:P * i + 2 * P, :].rearrange("(t p) c -> p t c", p=P), X[:, i:i + 2, :])\
                    .then_inc(out_done, 16)
            sp.wait_ge(out_done, 16 * (NT // 2))

        def pool_rest(pool, L, u, rows):
            z = sems[L]
            pool.wait_ge(z["hi_done"], u + 1)
            if u >= 2:
                pool.wait_ge(z["lo_done"], u - 1)
            pool.tensor_tensor(rest[0:rows, u % 2, :], rf[0:rows, u % 2, :], parts[0:rows, u % SLOTS, 0, :],
                               ALU.subtract).then_inc(z["rest_done"], 1)

        def pool_low(pool, L, u, rows):
            z = sems[L]
            pool.wait_ge(z["mid_done"], u + 1)
            pool.tensor_tensor(parts[0:rows, u % SLOTS, 2, :], rest[0:rows, u % 2, :], parts[0:rows, u % SLOTS, 1, :],
                               ALU.subtract).then_inc(z["lo_done"], 1)

        def pool_round(pool, g, half):
            z = sems[0]
            k = 2 * g + half
            w = raw[:, bass.ds(k + 1, 1), :].rearrange("p k n -> p (k n)")
            out_ = rounded[:, bass.ds(k, 1), 0:CW].rearrange("p k n -> p (k n)")
            a, b = tmpa, tmpb
            count = 0

            def step(ins):
                nonlocal count
                count += 1
                ins.then_inc(z["round_step"], 1)
                wait_count(pool, passed_pool, z["round_step"], ROUND_C + ROUND * k + count)

            wait_count(pool, passed_pool, z["power_done"], k + 1)
            step(pool.tensor_scalar(a, a, 2.0 ** -6, 1.5 * 2.0 ** 20, ALU.max, ALU.mult))
            step(pool.tensor_tensor(b, w, a, ALU.add))
            step(pool.tensor_tensor(w, b, a, ALU.subtract))
            step(pool.tensor_tensor(b, w, w, ALU.mult))
            step(pool.tensor_scalar(a, b, 448.0 ** 2, 3.0e38, ALU.is_gt, ALU.mult))
            step(pool.tensor_tensor(b, a, a, ALU.mult))
            step(pool.tensor_tensor(b, b, b, ALU.subtract))
            step(pool.tensor_tensor(out_, w, b, ALU.add))
            assert count == ROUND

        def pool_x_low(pool, T, c):
            z = sems[0]
            pool.wait_ge(z["xmid_done"], DC * T + c + 1)
            pool.tensor_tensor(xp[:, T % 2, c, 2, :], rest[:, c, :], xp[:, T % 2, c, 1, :], ALU.subtract)\
                .then_inc(z["xlow_done"], 1)

        def pool_h_low(pool, T, n):
            z = sems[0]
            k = FC[0] * T + n
            pool.wait_ge(z["hmid_done"], k + 1)
            pool.tensor_tensor(hp(T, 2, n), hrest[:, k % 2, :], hp(T, 1, n), ALU.subtract).then_inc(z["hid_done"], 1)

        def pool_shift(pool, L, n, T):
            z = sems[L]
            wait_count(pool, passed_pool, z["neg_max"], block_index(n, T) + 1)
            m = negm[:, T, :, :]

            def place(k):
                return sh[:, T % 2, HG * TB * k:HG * TB * k + HG * TB].rearrange("p (h t) -> p t h", t=TB)

            st = 3 * block_index(n, T) + 1
            pool.tensor_copy(place(0), m).then_inc(z["shift_step"], 1)
            wait_count(pool, passed_pool, z["shift_step"], st)
            pool.tensor_tensor(rm[:, :, :], m, place(0), ALU.subtract).then_inc(z["shift_step"], 1)
            wait_count(pool, passed_pool, z["shift_step"], st + 1)
            pool.tensor_copy(place(1), rm[:, :, :]).then_inc(z["shift_step"], 1)
            wait_count(pool, passed_pool, z["shift_step"], st + 2)
            pool.tensor_tensor(place(2), rm[:, :, :], place(1), ALU.subtract).then_inc(z["shift_done"], 1)

        @block.gpsimd
        def _(pool):
            pool.memset(ones_row[:, :], 1.0).then_inc(const_step, 1)
            pool.memset(ident[:, :], 0.0).then_inc(const_step, 1)
            pool.memset(mask_qk[:, :], 0.0).then_inc(const_step, 1)
            pool.memset(mask_kq[:, :], 0.0).then_inc(const_step, 1)
            pool.wait_ge(const_step, 4)
            pool.affine_select(out=ident[:, :], in_=ident[:, :], compare_op=ALU.not_equal, fill=1.0, base=0,
                               pattern=[[-1, P]], channel_multiplier=1).then_inc(const_step, 1)
            pool.affine_select(out=mask_qk[:, :], in_=mask_qk[:, :], compare_op=ALU.is_ge, fill=NEG, base=0,
                               pattern=[[-1, P]], channel_multiplier=1).then_inc(const_step, 1)
            pool.affine_select(out=mask_kq[:, :], in_=mask_kq[:, :], compare_op=ALU.is_ge, fill=NEG, base=0,
                               pattern=[[1, P]], channel_multiplier=-1).then_inc(const_step, 1)
            pool.wait_ge(const_step, 7)
            pool.tensor_copy(identb[:, :], ident[:, :]).then_inc(const_step, 1)
            pool.wait_ge(const_step, 8)
            pool.memset(KT2[6 * HD:6 * HD + PARTS, :, :, :].rearrange("p T h w -> p (T h w)"), 1.0).then_inc(fill_step, 1)
            pool.wait_ge(fill_step, 1)
            pool.memset(VG[:, :, :, HD:32].rearrange("p t h c -> p (t h) c"), 0.0).then_inc(fill_step, 1)
            pool.wait_ge(fill_step, 2)
            pool.memset(VG[:, :, :, HD:HD + 1].rearrange("p t h c -> p (t h) c"), 1.0).then_inc(fill_step, 1)
            for L in range(2):
                z = sems[L]
                for item in FIRST[L]:
                    what, T = item[0:2]
                    if what == "proj" and item[3] == 1:
                        j = item[2]
                        if L == 0:
                            pool_rest(pool, L, NPROJ[L] * T + j, PROJ[L][j][2])
                        if j > 0:
                            pool_low(pool, L, NPROJ[L] * T + j - 1, PROJ[L][j - 1][2])
                    elif what == "flush":
                        pool_low(pool, L, NPROJ[L] * (T + 1) - 1, PROJ[L][-1][2])
                    elif what == "split":
                        pool_shift(pool, L, 0, T)
                pool_shift(pool, L, 0, 2)
                if L == 0:
                    pool.sem_inc(z["round_step"], ROUND_C)
                with pool.Fori(0, NG - 1) as g:
                    if L == 0:
                        pool_round(pool, g, 0)
                    pool_shift(pool, L, g, TOP)
                    pool_shift(pool, L, g + 1, 0)
                    pool_shift(pool, L, g + 1, 1)
                    if L == 0:
                        pool_round(pool, g, 1)
                    pool_shift(pool, L, g + 1, 2)
                pool_shift(pool, L, NG - 1, TOP)
                if L == 0:
                    for item in LAST + AFTER[0]:
                        if item[0] == "xT":
                            pool_x_low(pool, *item[1:])
                        elif item[0] == "gu":
                            pool_h_low(pool, *item[1:])

        def pe_ring(pe, L, e):
            if not (isinstance(e, int) and e < len(RING)):
                pe.wait_ge(sems[L]["ring_read"], e - len(RING) + 1)

        def pe_unit(pe, L, n, unit, before, e, bank):
            z = sems[L]
            c, i, heads = unit
            w = width(c, i)
            fresh = before is None or before[1] // TB != i // TB
            if fresh or before[0] != c:
                pe.wait_ge(z["ak", c], AK * (n + 1))
            if fresh:
                pe.wait_ge(z["aq", i // TB], AQ * (n + 1))
            pe_ring(pe, L, e)
            diag = W * c + w == P * (i + 1)
            for k, h in enumerate(heads):
                hk = h if KH[L] > 1 else 0
                o = w * k
                last = pe.matmul(ps[:, bank, o:o + w], QT1[0:6 * HD, i // TB, h, P * (i % TB):P * (i % TB) + P],
                                 KT1[0:6 * HD, c, hk, 0:w], start=True, stop=not diag)
                if diag:
                    last = pe.matmul(ps[:, bank, o + w - P:o + w], identb[:, :], mask_qk[:, :],
                                     start=False, stop=True)
            last.then_inc(z["ring_ready"], 1)

        def pe_scores(pe, L, g, q, pair):
            z = sems[L]
            T, j, off = QUADS[q]
            c = j // TB
            if pair == 0 and j == 0:
                pe.wait_ge(z["bq", T], BQ * (g + 1))
            if pair == 0 and T == c and j == TB * c:
                pe.wait_ge(z["bk", c], BK * (g + 1))
            pe.wait_ge(z["exp_done"], EXP_C + 2 * (NQ * g + q) + pair - 1)
            for h in (2 * pair, 2 * pair + 1):
                hk = h if KH[L] > 1 else 0
                diag = j >= TB * T
                last = pe.matmul(ps[:, h, off:W], KT2[0:6 * HD + PARTS, c, hk, P * (j % TB):P * (j % TB) + P],
                                 QT2[0:6 * HD + PARTS, T, h, off:W], start=True, stop=not diag)
                if diag:
                    last = pe.matmul(ps[:, h, off:off + P], identb[:, :], mask_kq[:, :], start=False, stop=True)
            last.then_inc(z["s_ready"], 1)

        def pe_pv(pe, L, g, q):
            z = sems[L]
            T, j, off = QUADS[q]
            first = j == 0
            if first:
                pe.wait_ge(z["ot_copied"], OTC_C + NB * g + T)
            pe.wait_ge(z["exp_done"], EXP_C + 2 * (NQ * g + q) + 2)
            for h in range(HG):
                hk = h if KH[L] > 1 else 0
                last = pe.matmul(ps[32 * h:32 * h + 32, ACC, off:W], VG[:, j, hk, :], PB[:, q % 2, h, off:W],
                                 start=first, stop=q == T_END[T])
            last.then_inc(z["pv_done"], 1)

        def pe_shift(pe, L, n, T, e, bank):
            z = sems[L]
            pe.wait_ge(z["shift_done"], block_index(n, T) + 1)
            pe_ring(pe, L, e)
            pe.matmul(ps[0:PARTS * HG * TB, bank, 0:P], sh[:, T % 2, :], identb[:, :], start=True, stop=True)\
                .then_inc(z["ring_ready"], 1)

        def pe_turn(pe, L, g, T, e, bank):
            z = sems[L]
            pe.wait_ge(z["ot_copied"], OTC_C + NB * g + T + 1)
            pe_ring(pe, L, e)
            for t in range(TB):
                last = pe.transpose(ps[:, bank, P * t:P * t + P], OT[:, T % 2, P * t:P * t + P], ident[:, :])
            last.then_inc(z["ring_ready"], 1)

        def pe_stage(pe, L, g, plan, base):
            e = 0
            before = None
            for item in plan:
                what, k = item[0:2]
                if what == "scores":
                    pe_scores(pe, L, g, k, item[2])
                elif what == "pv":
                    pe_pv(pe, L, g, k)
                elif what in RINGED:
                    bank = RING[(NFIRST + e) % len(RING)]
                    if what == "shift":
                        pe_shift(pe, L, g if k >= 2 else g + 1, k, base + e, bank)
                    elif what == "unit":
                        pe_unit(pe, L, g if k < NHIGH else g + 1, UNITS[k], before, base + e, bank)
                        before = UNITS[k]
                    elif what == "turn":
                        pe_turn(pe, L, g, k, base + e, bank)
                    else:
                        pe_dense(pe, L, item)
                    e += 1

        def pe_project(pe, L, T, j, half):
            z = sems[L]
            first, swapped, rows = PROJ[L][j]
            if j == 0 and half == 0:
                if L == 0:
                    pe.wait_ge(xT_in[T], 16 * DC)
                else:
                    pe.wait_ge(sems[0]["ring_read"], tail_entry(0, "x2T", T, 1))
                    if T == 0:
                        pe.wait_ge(sems[0]["h_done"], FC[0] * NB)
            u = NPROJ[L] * T + j
            slots = (2, 4)[L]
            if half == 0 and u >= slots:
                pe.wait_ge(z["proj_read"], u - slots + 1)
            b = u % slots * (4 // slots)
            if L == 0:
                b, col = b + half, (first, swapped)[half]
            else:
                col = first
            for c in range(DC) if L == 0 else (half,):
                last = pe.matmul(ps[0:rows, b, :], wqkv[:, c, col:col + rows], xT[:, c, W * T:W * T + W],
                                 start=c == 0, stop=c == DC - 1)
            if half == 1:
                last.then_inc(z["proj_ready"], 1)

        def pe_values(pe, L, T, half):
            z = sems[L]
            if 2 * T + half >= 1:
                pe.wait_ge(z["v_copied"], 2 * T + half)
            for t in range(2):
                i = TB * T + 2 * half + t
                dst = ps[:, ACC, KV[L] * t:KV[L] * t + KV[L]]
                for c in range(DC):
                    last = pe.matmul(dst, xT[:, c, P * i:P * i + P], wqkv[:, c, VOFF[L]:VOFF[L] + KV[L]],
                                     start=c == 0, stop=L == 1 and c == DC - 1)
                if L == 0:
                    last = pe.matmul(dst, ones_row[:, :], bv[:, :], start=False, stop=True)
            last.then_inc(z["v_ready"], 1)

        def pe_dense(pe, L, item):
            z = sems[L]
            what, T, k = item
            e = tail_entry(L, *item) - 1
            bank = RING[e % len(RING)]
            if what == "oT":
                pe.wait_ge(z["ring_read"], tail_entry(L, "turn", T))
            elif what == "y":
                if T == 0 and k == 0:
                    pe.wait_ge(z["wload"], 16 if L == 0 else 48)
                    if L == 0:
                        pe.wait_ge(b_in, 64)
                pe.wait_ge(z["ring_read"], tail_entry(L, "oT", T, 1))
            elif what == "xT":
                pe.wait_ge(z["ln_done"], TB * (T + 1))
            elif what == "down":
                pe.wait_ge(z["hid_done"], FC[L] * (T + 1))
            elif what == "x2T":
                pe.wait_ge(z["ln2_done"], TB * (T + 1))
            pe_ring(pe, L, e)
            if what in ("oT", "xT", "x2T"):
                src = O if what == "oT" else X
                for t in range(TB):
                    last = pe.transpose(ps[:, bank, P * t:P * t + P], src[:, TB * T + t, P * k:P * k + P],
                                        ident[:, :])
            for t in (2 * k, 2 * k + 1):
                dst = ps[:, bank, D * (t % 2):D * (t % 2) + D]
                i = TB * T + t
                if what == "y":
                    for c in range(DC):
                        last = pe.matmul(dst, xT[:, c, P * i:P * i + P], wo[:, c, :],
                                         start=c == 0, stop=L == 1 and c == DC - 1)
                    if L == 0:
                        last = pe.matmul(dst, ones_row[:, :], bo[:, :], start=False, stop=True)
                elif what == "down" and L == 0:
                    for n in range(FC[0]):
                        at = DC * D // 2 * n
                        for part in range(PARTS):
                            last = pe.matmul(dst, hp(T, part, n)[:, P * t:P * t + P],
                                             rounded[:, 4 + at // CW, at % CW:at % CW + D],
                                             start=n == 0 and part == 0, stop=n == FC[0] - 1 and part == PARTS - 1)
                elif what == "down":
                    for n in range(FC[L]):
                        last = pe.matmul(dst, hid[T % 2][:, n, P * t:P * t + P], WD[:, n, :],
                                         start=n == 0, stop=n == FC[L] - 1)
            last.then_inc(z["ring_ready"], 1)

        def pe_hidden(pe, L, T, n):
            z = sems[L]
            if n == 0 and L == 0:
                pe.wait_ge(z["xlow_done"], DC * (T + 1))
            elif n == 0:
                pe.wait_ge(z["ring_read"], tail_entry(L, "xT", T, 1))
            if T == 0 and n == 0:
                if L == 0:
                    pe.wait_ge(z["round_step"], ROUND_C + ROUND * CHUNKS)
                else:
                    pe.wait_ge(z["ffw"], 48)
            k = FC[L] * T + n
            b = 2 * (k % 2)
            if k >= 2:
                pe.wait_ge(z["h_done" if L == 0 else "hid_done"], k - 1)
            for o in range(2):
                for c in range(DC):
                    if L == 0:
                        for part in range(PARTS):
                            last = pe.matmul(ps[:, b + o, :], rounded[:, DC * o + c, P * n:P * n + P],
                                             xp[:, T % 2, c, part, :], start=c == 0 and part == 0,
                                             stop=c == DC - 1 and part == PARTS - 1)
                    else:
                        last = pe.matmul(ps[:, b + o, :], (WG, WU)[o][:, c, P * n:P * n + P],
                                         xT[:, c, W * T:W * T + W], start=c == 0, stop=c == DC - 1)
            last.then_inc(z["gu_ready"], 1)

        def pe_behind(pe, L, plan):
            for item in plan:
                if item[0] == "gu":
                    pe_hidden(pe, L, *item[1:])
                elif item[0] not in RINGED:
                    continue
                elif item[0] == "turn":
                    e = tail_entry(L, *item) - 1
                    pe_turn(pe, L, NG - 1, TOP, e, RING[e % len(RING)])
                else:
                    pe_dense(pe, L, item)

        @block.tensor
        def _(pe):
            pe.wait_ge(const_step, 8)
            pe.wait_ge(w_in, 16 * (DC + 2))
            for L in range(2):
                z = sems[L]
                pe.sem_inc(z["pv_done"], PV_C)
                if L == 1:
                    pe.wait_ge(z["wload"], 16 * DC)
                for item in FIRST[L]:
                    what, k = item[0:2]
                    if what == "proj":
                        pe_project(pe, L, k, *item[2:])
                    elif what == "values":
                        pe_values(pe, L, k, item[2])
                    elif what in ("low", "shift"):
                        e = first_entry(*item) - 1
                        bank = RING[e % len(RING)]
                        if L == 1 and e == 0:
                            pe.wait_ge(sems[0]["ring_read"], BASE_LAST + len(TAIL[0]))
                        if what == "low":
                            pe_unit(pe, L, 0, LOW[k], LOW[k - 1] if k else None, e, bank)
                        else:
                            pe_shift(pe, L, 0, k, e, bank)
                    elif what in RINGED:
                        pe_dense(pe, 0, item)
                with pe.Fori(0, NG - 1) as g:
                    pe_stage(pe, L, g, STAGE, NFIRST + NE * g)
                pe_stage(pe, L, NG - 1, LAST, BASE_LAST)
                pe_behind(pe, L, AFTER[L])

        def act_sqrt(act, L, what, T):
            z = sems[L]
            second = what == "sqrt2"
            rs = rstd[:, int(second), TB * T:TB * T + TB]
            act.wait_ge(z["var2_done" if second else "var_done"], T + 1)
            act.activation(rs, rs, ACT.Sqrt).then_inc(z["sqrt2_done" if second else "sqrt_done"], 1)

        def act_stage(act, L, g, plan, base):
            z = sems[L]
            for q in range(NQ):
                T, j, off = QUADS[q]
                for pair in range(2):
                    act.wait_ge(z["s_ready"], 2 * (NQ * g + q) + pair + 1)
                    if pair == 0:
                        act.wait_ge(z["pv_done"], PV_C + NQ * g + q - 1)
                    act.activation(PB[:, q % 2, 2 * pair:2 * pair + 2, off:W], ps[:, 2 * pair:2 * pair + 2, off:W],
                                   ACT.Exp, scale=SCALE).then_inc(z["exp_done"], 1)
                if plan is LAST:
                    for item in DENSE_AT.get(q, []):
                        if item[0] == "sqrt":
                            act_sqrt(act, L, *item)
                done = [t for t in range(NB) if q == min(T_END[t] + 1, NQ - 1)]
                for t in done:
                    act.wait_ge(z["pv_done"], PV_C + NQ * g + T_END[t] + 1)
                    act.wait_ge(z["ring_ready"], base + entry_after(plan, "turn", t - 2) if t >= 2 else base)
                    act.activation(OT[:, t % 2, :], ps[:, ACC, :], ACT.Copy).then_inc(z["ot_copied"], 1)

        def act_middle(act, L, u, rows):
            z = sems[L]
            act.wait_ge(z["rest_done" if L == 0 else "proj_read"], u + 1)
            act.activation(parts[0:rows, u % SLOTS, 1, :], rest[0:rows, u % 2, :], ACT.Copy).then_inc(z["mid_done"], 1)

        def act_store(act, L, T, j):
            z = sems[L]
            u = NPROJ[L] * T + j
            dst, c = (q_s, j) if j < DC else (k_s, j - DC)
            dst = dst[L].rearrange("g h r s -> (g h) r s")
            rows = PROJ[L][j][2]
            act.wait_ge(z["lo_done"], u + 1)
            for k in range(PARTS):
                act.dma_start(dst[P // HD * c:P // HD * c + rows // HD, HD * k:HD * k + HD, W * T:W * T + W],
                              parts[0:rows, u % SLOTS, k, :]).then_inc(z["stored"][u % SLOTS], 16)

        def act_project(act, L, T, j):
            z = sems[L]
            rows = PROJ[L][j][2]
            u = NPROJ[L] * T + j
            if L == 0:
                act.wait_ge(z["rope_f"], u + 1)
                src = rf[0:rows, u % 2, :]
            else:
                act.wait_ge(z["proj_ready"], u + 1)
                src = ps[0:rows, u % 4, :]
            if L == 1 and u == 0:
                act.wait_ge(sems[0]["hid_done"], FC[0] * NB)
            if u >= SLOTS:
                act.wait_ge(z["stored"][u % SLOTS], 16 * PARTS * (u // SLOTS))
            act.activation(parts[0:rows, u % SLOTS, 0, :], src, ACT.Copy).then_inc(z["hi_done"], 1)
            if j > 0:
                act_middle(act, L, u - 1, PROJ[L][j - 1][2])
            if j > 1:
                act_store(act, L, T, j - 2)

        def act_values(act, L, T, half):
            z = sems[L]
            if half == 0 and T > 0:
                act.wait_ge(z["v_stored"], 16 * T)
            act.wait_ge(z["v_ready"], 2 * T + half + 1)
            act.activation(vrow[:, 2 * half:2 * half + 2, 0:KV[L]],
                           ps[:, ACC, 0:2 * KV[L]].rearrange("p (t c) -> p t c", t=2), ACT.Copy)\
                .then_inc(z["v_copied"], 1)
            if half == 1:
                act.wait_ge(z["v_copied"], 2 * (T + 1))
                act.dma_start(v_s[L][W * T:W * T + W, :].rearrange("(t p) c -> p t c", p=P), vrow[:, :, 0:KV[L]])\
                    .then_inc(z["v_stored"], 16)

        @block.scalar
        def _(act):
            for L in range(2):
                z = sems[L]
                act.sem_inc(z["exp_done"], EXP_C)
                act.sem_inc(z["ot_copied"], OTC_C)
                for item in FIRST[L]:
                    if item[0] == "proj" and item[3] == 1:
                        act_project(act, L, *item[1:3])
                    elif item[0] == "values":
                        act_values(act, L, *item[1:])
                    elif item[0] == "flush":
                        act_middle(act, L, NPROJ[L] * (item[1] + 1) - 1, PROJ[L][-1][2])
                        act_store(act, L, item[1], NPROJ[L] - 2)
                        act_store(act, L, item[1], NPROJ[L] - 1)
                    elif item[0] == "sqrt2":
                        act_sqrt(act, 0, *item)
                with act.Fori(0, NG - 1) as g:
                    act_stage(act, L, g, STAGE, NFIRST + NE * g)
                act_stage(act, L, NG - 1, LAST, BASE_LAST)
                for item in AFTER[L]:
                    if item[0] in ("sqrt", "sqrt2"):
                        act_sqrt(act, L, *item)
                    if item[0] != "gu":
                        continue
                    T, n = item[1:]
                    k = FC[L] * T + n
                    act.wait_ge(z["gu_ready"], k + 1)
                    if k >= 2:
                        act.wait_ge(z["h_done" if L == 0 else "hid_done"], k - 1)
                    act.activation(sl[:, k % 2, :], ps[:, 2 * (k % 2), :], ACT.Silu,
                                   scale=gs[:, n:n + 1] if L == 0 else 1.0).then_inc(z["silu_done"], 1)
                    if L == 0:
                        if n == 0 and T >= 2:
                            act.wait_ge(z["ring_ready"], tail_entry(0, "down", T - 2, 1))
                        act.wait_ge(z["h_done"], k + 1)
                        act.activation(hp(T, 0, n), hf[:, k % 2, :], ACT.Copy).then_inc(z["hhigh_done"], 1)
                        act.wait_ge(z["hrest_done"], k + 1)
                        act.activation(hp(T, 1, n), hrest[:, k % 2, :], ACT.Copy).then_inc(z["hmid_done"], 1)

        def dve_project(dve, L, T, j):
            z = sems[L]
            rows = PROJ[L][j][2]
            u = NPROJ[L] * T + j
            dve.wait_ge(z["proj_ready"], u + 1)
            if L == 1:
                dve.wait_ge(z["hi_done"], u + 1)
                if u >= 2:
                    dve.wait_ge(z["lo_done"], u - 1)
                dve.tensor_tensor(rest[0:rows, u % 2, :], ps[0:rows, u % 4, :], parts[0:rows, u % SLOTS, 0, :],
                                  ALU.subtract).then_inc(z["proj_read"], 1)
                return
            if j == 0:
                dve.wait_ge(rope_in[T], 16)
                if T == 0:
                    dve.wait_ge(w_in, 16 * (DC + 2))
            if u >= 1:
                dve.wait_ge(z["rope_f"], u)
            b = 2 * (u % 2)
            dve.scalar_tensor_tensor(out=ra[0:rows, :], in0=ps[0:rows, b, :], scalar=bqk[0:rows, j:j + 1],
                                     in1=rope[0:rows, 0, W * T:W * T + W], op0=ALU.add, op1=ALU.mult)\
                .then_inc(z["rope_a"], 1)
            dve.scalar_tensor_tensor(out=rb[0:rows, :], in0=ps[0:rows, b + 1, :],
                                     scalar=bqk[0:rows, NPROJ[0] + j:NPROJ[0] + j + 1],
                                     in1=rope[0:rows, 1, W * T:W * T + W], op0=ALU.add, op1=ALU.mult)\
                .then_inc(z["proj_read"], 1)
            dve.wait_ge(z["rope_a"], u + 1)
            dve.wait_ge(z["proj_read"], u + 1)
            if u >= 2:
                dve.wait_ge(z["rest_done"], u - 1)
            dve.tensor_tensor(rf[0:rows, u % 2, :], ra[0:rows, :], rb[0:rows, :], ALU.add).then_inc(z["rope_f"], 1)

        def dve_shift(dve, L, n, T, e, bank):
            z = sems[L]
            dve.wait_ge(z["ring_ready"], e + 1)
            if T >= 2:
                dve.wait_ge(z["bq", T - 2], BQ * (n + 1))
            elif not (isinstance(n, int) and n == 0):
                dve.wait_ge(z["bq", T + 2], BQ * n)
            dve.tensor_copy(shT[:, T % 2, :], ps[0:PARTS * HG * TB, bank, 0:P]).then_inc(z["ring_read"], 1)

        def dve_unit(dve, L, unit, e, bank):
            z = sems[L]
            c, i, heads = unit
            w = width(c, i)
            dve.wait_ge(z["ring_ready"], e + 1)
            dve.tensor_reduce(pm[:, i // TB, i % TB, heads[0]:heads[-1] + 1, c],
                              ps[:, bank, 0:w * len(heads)].rearrange("p (h w) -> p h w", w=w), AX.X, ALU.max)\
                .then_inc(z["ring_read"], 1)

        def dve_neg_max(dve, L, n, T, entries):
            z = sems[L]
            dve.wait_ge(z["ring_read"], entries)
            if not (isinstance(n, int) and n == 0):
                dve.wait_ge(z["shift_done"], block_index(n - 1, T) + 1)
            dve.tensor_reduce(negm[:, T, :, :], pm[:, T, :, :, 0:T + 1], AX.X, ALU.max, negate=True)\
                .then_inc(z["neg_max"], 1)

        def dve_norm(dve, L, g, T, e, bank):
            z = sems[L]
            tr = ps[:, bank, :].rearrange("p (t h c) -> p t h c", t=TB, h=HG)
            dve.wait_ge(z["ring_ready"], e + 1)
            dve.reciprocal(rden[:, T, :, :], tr[:, :, :, HD]).then_inc(z["o_step"], 1)
            dve.wait_ge(z["o_step"], NB * g + T + 1)
            dve.tensor_tensor(O[:, TB * T:TB * T + TB, bass.ds(g * (HG * HD), HG * HD)]
                              .rearrange("p t (h d) -> p t h d", d=HD), tr[:, :, :, 0:HD],
                              rden[:, T, :, :, None].to_broadcast([P, TB, HG, HD]), ALU.mult).then_inc(z["ring_read"], 1)

        def dve_power(dve, g, half):
            k = 2 * g + half
            dve.wait_ge(sems[0]["ffw"], 48)
            dve.wait_ge(sems[0]["round_step"], ROUND_C + ROUND * k)
            dve.tensor_scalar(tmpa.bitcast(INT32), raw[:, bass.ds(k + 1, 1), :].rearrange("p k n -> p (k n)").bitcast(INT32),
                              0x7F800000, None, ALU.bitwise_and).then_inc(sems[0]["power_done"], 1)

        def dve_stage(dve, L, g, plan, base, steps):
            e = 0
            for item in plan:
                what, k = item[0:2]
                if what == "ln":
                    dve_layernorm(dve, L, what, k, steps)
                if plan is STAGE and L == 0 and item in POWERS:
                    dve_power(dve, g, POWERS.index(item))
                if what not in RINGED:
                    continue
                bank = RING[(NFIRST + e) % len(RING)]
                if what == "shift":
                    dve_shift(dve, L, g if k >= 2 else g + 1, k, base + e, bank)
                elif what == "turn":
                    dve_norm(dve, L, g, k, base + e, bank)
                elif what == "unit":
                    dve_unit(dve, L, UNITS[k], base + e, bank)
                    T = UNITS[k][1] // TB
                    if k + 1 == len(UNITS) or UNITS[k + 1][1] // TB != T:
                        dve_neg_max(dve, L, g if T == TOP else g + 1, T, base + e + 1)
                else:
                    dve_dense(dve, L, item, steps)
                e += 1

        def in_step(dve, L, steps, ins):
            steps[L] += 1
            ins.then_inc(sems[L]["ln_step"], 1)
            dve.wait_ge(sems[L]["ln_step"], steps[L])

        def dve_statistics(dve, L, T, half, second, steps):
            i = TB * T + 2 * half
            for t in (i, i + 1):
                in_step(dve, L, steps, dve.bn_stats(stats[:, t, :], X[:, t, :]))
                in_step(dve, L, steps, dve.bn_aggr(mv[:, t, :], stats[:, t, :]))
            if half == 1:
                dve.tensor_scalar(rstd[:, int(second), TB * T:TB * T + TB], mv[:, TB * T:TB * T + TB, 1], EPS, None,
                                  ALU.add).then_inc(sems[L]["var2_done" if second else "var_done"], 1)

        def dve_layernorm(dve, L, what, T, steps):
            z = sems[L]
            second = what == "ln2"
            rs = rstd[:, int(second), :]
            dve.wait_ge(z["sqrt2_done" if second else "sqrt_done"], T + 1)
            in_step(dve, L, steps, dve.reciprocal(rs[:, TB * T:TB * T + TB], rs[:, TB * T:TB * T + TB]))
            for t in range(TB * T, TB * T + TB):
                dve.tensor_scalar(X[:, t, :], X[:, t, :], mv[:, t, 0:1], rs[:, t:t + 1], ALU.subtract, ALU.mult)\
                    .then_inc(z["ln2_done" if second else "ln_done"], 1)

        def dve_dense(dve, L, item, steps):
            z = sems[L]
            what, T, k = item
            e = tail_entry(L, *item) - 1
            bank = RING[e % len(RING)]
            dve.wait_ge(z["ring_ready"], e + 1)
            if what == "xT" and L == 0:
                if T == 0 and k == 0:
                    dve.wait_ge(z["bk", TOP], BK * NG)
                    dve.wait_ge(z["bq", TOP], BQ * NG)
                if T >= 1:
                    dve.wait_ge(z["xlow_done"], DC * (T - 1) + k + 1)
                in_step(dve, L, steps, dve.tensor_copy(xp[:, T % 2, k, 0, :], ps[:, bank, :]))
                dve.tensor_tensor(rest[:, k, :], ps[:, bank, :], xp[:, T % 2, k, 0, :], ALU.subtract)\
                    .then_inc(z["ring_read"], 1)
                dve.wait_ge(z["ring_read"], e + 1)
                dve.tensor_copy(xp[:, T % 2, k, 1, :], rest[:, k, :]).then_inc(z["xmid_done"], 1)
                return
            if what in ("oT", "xT", "x2T"):
                dve.tensor_copy(xT[:, k, W * T:W * T + W], ps[:, bank, :]).then_inc(z["ring_read"], 1)
                return
            i = TB * T + 2 * k
            y = ps[:, bank, :].rearrange("p (t c) -> p t c", t=2)
            if what == "down" and L == 0:
                dve.tensor_tensor(yt[:, :, :], y, ds[:, None, :].to_broadcast([P, 2, D]), ALU.mult)\
                    .then_inc(z["ring_read"], 1)
                dve.wait_ge(z["ring_read"], e + 1)
                in_step(dve, L, steps, dve.tensor_tensor(X[:, i:i + 2, :], yt[:, :, :], X[:, i:i + 2, :], ALU.add))
            else:
                if L == 0 and T == 0 and k == 0:
                    dve.wait_ge(x_in, 16)
                dve.tensor_tensor(X[:, i:i + 2, :], y, X[:, i:i + 2, :], ALU.add).then_inc(z["ring_read"], 1)
                dve.wait_ge(z["ring_read"], e + 1)
            dve_statistics(dve, L, T, k, what == "down", steps)

        def dve_hidden(dve, L, T, n):
            z = sems[L]
            k = FC[L] * T + n
            if L == 1 and n == 0 and T >= 2:
                dve.wait_ge(z["ring_ready"], tail_entry(L, "down", T - 2, 1))
            dve.wait_ge(z["silu_done"], k + 1)
            dve.wait_ge(z["gu_ready"], k + 1)
            up = ps[:, 2 * (k % 2) + 1, :]
            if L == 0:
                dve.scalar_tensor_tensor(out=hf[:, k % 2, :], in0=up, scalar=us[:, n:n + 1],
                                         in1=sl[:, k % 2, :], op0=ALU.mult, op1=ALU.mult)\
                    .then_inc(z["h_done"], 1)
                if k >= 2:
                    dve.wait_ge(z["hid_done"], k - 1)
                dve.wait_ge(z["hhigh_done"], k + 1)
                dve.tensor_tensor(hrest[:, k % 2, :], hf[:, k % 2, :], hp(T, 0, n), ALU.subtract)\
                    .then_inc(z["hrest_done"], 1)
            else:
                dve.tensor_tensor(hid[T % 2][:, n, :], up, sl[:, k % 2, :], ALU.mult).then_inc(z["hid_done"], 1)

        @block.vector
        def _(dve):
            steps = [0, 0]
            for L in range(2):
                z = sems[L]
                for item in FIRST[L]:
                    what, k = item[0:2]
                    if what == "proj" and item[3] == 1:
                        dve_project(dve, L, k, item[2])
                    elif what in ("low", "shift"):
                        e = first_entry(*item) - 1
                        bank = RING[e % len(RING)]
                        if what == "shift":
                            dve_shift(dve, L, 0, k, e, bank)
                            continue
                        dve_unit(dve, L, LOW[k], e, bank)
                        T = LOW[k][1] // TB
                        if k + 1 == len(LOW) or LOW[k + 1][1] // TB != T:
                            dve_neg_max(dve, L, 0, T, e + 1)
                    elif what == "ln2":
                        dve_layernorm(dve, 0, what, k, steps)
                    elif what in RINGED:
                        dve_dense(dve, 0, item, steps)
                with dve.Fori(0, NG - 1) as g:
                    dve_stage(dve, L, g, STAGE, NFIRST + NE * g, steps)
                dve_stage(dve, L, NG - 1, LAST, BASE_LAST, steps)
                for item in AFTER[L]:
                    if item[0] == "gu":
                        dve_hidden(dve, L, *item[1:])
                    elif item[0] == "turn":
                        e = tail_entry(L, *item) - 1
                        dve_norm(dve, L, NG - 1, TOP, e, RING[e % len(RING)])
                    elif item[0] in RINGED:
                        dve_dense(dve, L, item, steps)
                    elif item[0] in ("ln", "ln2"):
                        dve_layernorm(dve, L, *item, steps)


def _rope_table():
    inv_freq = np.float32(1.0) / np.power(np.float32(10000.0), np.arange(0, HD, 2, dtype=np.float32) / np.float32(HD))
    angle = np.arange(S, dtype=np.float32)[:, None] * inv_freq[None, :].astype(np.float32)
    cos, sin = np.cos(angle), np.sin(angle)
    rows = np.stack([np.repeat(cos, 2, axis=1).T, np.stack([-sin, sin], axis=-1).reshape(S, HD).T], axis=1)
    return np.tile(rows, (P // HD, 1, 1)).astype(np.float32)


def _swapped(a):
    return a.reshape(a.shape[0], -1, 2)[:, :, ::-1].reshape(a.shape)


def _biases(bq, bk):
    rows = np.concatenate([bq, bk])[None, :]
    out = np.zeros((2 * NPROJ[0], P), np.float32)
    for o, r in enumerate((rows[0], _swapped(rows)[0])):
        for j, (first, _, n) in enumerate(PROJ[0]):
            out[NPROJ[0] * o + j, 0:n] = r[first:first + n]
    return out.T


def kernel(**inputs):
    import concourse.bacc as _bacc
    from concourse import mybir as _mybir
    from concourse.bass_utils import run_bass_kernel_spmd as _run

    i = inputs
    host = {
        "x": i["L0_attn_x"][0],
        "xT": i["L0_attn_x"][0].T,
        "wqkv0": np.concatenate([i["L0_attn_Wq"].T, i["L0_attn_Wk"].T, i["L0_attn_Wv"].T,
                                 _swapped(i["L0_attn_Wq"].T), _swapped(i["L0_attn_Wk"].T)], axis=1),
        "wqkv1": np.concatenate([i["L1_attn_wq"].T, i["L1_attn_wk"].T, i["L1_attn_wv"].T], axis=1),
        "bqk": _biases(i["L0_attn_bq"], i["L0_attn_bk"]),
        "bv": i["L0_attn_bv"][None, :],
        "wo0": i["L0_attn_Wo"].T,
        "wo1": i["L1_attn_wo"].T,
        "bo": i["L0_attn_bo"][None, :],
        "gate0": i["L0_ffn_gate_w"],
        "gate1": i["L1_ffn_w_gate"].T,
        "up0": i["L0_ffn_up_w"],
        "up1": i["L1_ffn_w_up"].T,
        "down0": i["L0_ffn_down_w"],
        "down1": i["L1_ffn_w_down"].T,
        "gs": i["L0_ffn_gate_scale"].reshape(FC[0], P).T,
        "us": i["L0_ffn_up_scale"].reshape(FC[0], P).T,
        "ds": i["L0_ffn_down_scale"][None, :],
        "rope": _rope_table(),
    }
    nc = _bacc.Bacc("TRN2", target_bir_lowering=False, num_devices=1)
    arrays, t = {}, {}
    for name, a in host.items():
        a = np.ascontiguousarray(a)
        arrays[f"in_{name}_dram"] = a
        t[name] = nc.dram_tensor(f"in_{name}_dram", a.shape, _mybir.dt.from_np(a.dtype), kind="ExternalInput").ap()
    out = nc.dram_tensor("out_0_dram", (1, S, D), FP32, kind="ExternalOutput").ap()
    network_kernel(nc, t["x"], t["xT"], (t["wqkv0"], t["wqkv1"]), t["bqk"], t["bv"], (t["wo0"], t["wo1"]), t["bo"],
                   (t["gate0"], t["gate1"]), (t["up0"], t["up1"]), (t["down0"], t["down1"]), t["gs"], t["us"],
                   t["ds"], t["rope"], out[0])
    r = _run(nc, [arrays], core_ids=[0])
    return r.results[0]["out_0_dram"]
```
